# Optimizing a Trainium2 kernel written in Bass

```python
import numpy as np
import jax
import jax.numpy as jnp

def _softmax(x, axis=-1):
    return jax.nn.softmax(x, axis=axis)

def _gelu(x):
    return jax.nn.gelu(x, approximate=True)

def _silu(x):
    return jax.nn.silu(x)

def _sigmoid(x):
    return jax.nn.sigmoid(x)

def _layernorm(x, axis=-1, eps=1e-05):
    m = jnp.mean(x, axis=axis, keepdims=True)
    v = jnp.var(x, axis=axis, keepdims=True)
    return (x - m) / jnp.sqrt(v + eps)

def _scatter_add(tgt, idx, src, axis=0):
    return tgt.at[idx].add(src)

def _segment_sum(src, seg, n):
    return jax.ops.segment_sum(src, seg, n)
kernel_name = 'mk_flamingo_gated_d2_seqx_r4_d79ab9'

def setup_inputs(seed: int=0):
    np.random.seed(seed)
    _w = jnp.asarray

    def _rec_inputs():
        import jax
        import jax.numpy as jnp
        _rk = jax.random.key(seed)
        x = -0.0002928 + 1 * jax.random.normal(jax.random.fold_in(_rk, 1), (16, 256, 256), jnp.float32)
        _lenS = 256 - jax.random.randint(jax.random.fold_in(_rk, 7), (16,), 0, max(1, 256 // 4) + 1, jnp.int32)
        _lenS2 = 77 - jax.random.randint(jax.random.fold_in(_rk, 8), (16,), 0, max(1, 77 // 4) + 1, jnp.int32)
        _ctx_1024P = jax.random.normal(jax.random.fold_in(_rk, 11), (16, 16, 256), jnp.float32)
        _ctx_1024c = jax.random.dirichlet(jax.random.fold_in(_rk, 511), 0.3 * jnp.ones((16,), jnp.float32), (16, 77))
        _ctx_1024t = jnp.einsum('bsk,bkd->bsd', _ctx_1024c, _ctx_1024P)
        _ctx_1024t = _ctx_1024t * jax.lax.rsqrt(jnp.mean(jnp.square(_ctx_1024t)) + 1e-12) * 0.953939
        ctx_1024 = -1.39393e-06 + 0.999914 * (_ctx_1024t + 0.3 * jax.random.normal(jax.random.fold_in(_rk, 611), (16, 77, 256), jnp.float32))
        _validS = jnp.arange(256)[None, :] < _lenS[:, None]
        _validS2 = jnp.arange(77)[None, :] < _lenS2[:, None]
        _causal = jnp.tril(jnp.ones((256, 256), dtype=bool))
        mask_Bx1xSxS2_if1 = jnp.where(jnp.ones((16, 1, 256, 77), dtype=bool), 1, 0).astype(jnp.int32)
        mask_1x1xSxS2_ik0 = jnp.where(jnp.broadcast_to(_validS2[0:1, None, None, :], (1, 1, 256, 77)), 0, 1).astype(jnp.int32)
        _g = jax.random.normal(jax.random.fold_in(_rk, 9001), (2, 2), jnp.float32)
        _g = jnp.sign(_g) * jnp.maximum(jnp.abs(_g), 1.0) + (_g == 0) * 1.0
        g_xattn = _g[0]
        g_ffn = _g[1]
        return (x, ctx_1024, mask_Bx1xSxS2_if1, mask_1x1xSxS2_ik0, g_xattn, g_ffn)
    x, ctx_1024, mask_Bx1xSxS2_if1, mask_1x1xSxS2_ik0, g_xattn, g_ffn = _rec_inputs()

    def _L0_xattn_setup():
        import jax, jax.numpy as jnp
        import numpy as np
        from math import sqrt
        H = 16
        key = jax.random.key(seed)
        ks = jax.random.split(key, 8)
        B, Sq, Skv, Dq, Dkv, Dall = (2, 512, 512, 256, 256, 256)
        x = jax.random.normal(ks[0], (B, Sq, Dq), dtype=jnp.float32)
        y = jax.random.normal(ks[1], (B, Skv, Dkv), dtype=jnp.float32)
        attention_mask = jnp.ones((B, 1, Sq, Skv), dtype=jnp.int32)
        Wq = jax.random.normal(ks[2], (Dall, Dq), dtype=jnp.float32) * 0.02
        Wk = jax.random.normal(ks[3], (Dall, Dkv), dtype=jnp.float32) * 0.02
        Wv = jax.random.normal(ks[4], (Dall, Dkv), dtype=jnp.float32) * 0.02
        Wo = jax.random.normal(ks[5], (Dq, Dall), dtype=jnp.float32) * 0.02
        bo = jnp.zeros((Dq,), dtype=jnp.float32)
        return {'x': x, 'y': y, 'attention_mask': attention_mask, 'Wq': Wq, 'Wk': Wk, 'Wv': Wv, 'Wo': Wo, 'bo': bo}
    _L0_xattn_all = _L0_xattn_setup()
    _L0_xattn_in = {k: v for k, v in _L0_xattn_all.items() if k in ('Wq', 'Wk', 'Wv', 'Wo', 'bo')}
    del _L0_xattn_all

    def _L0_ffn_setup():
        import jax, jax.numpy as jnp
        import numpy as np
        H = 256
        F = 1024
        E = 8
        TOP_K = 2
        B, S = (1, 512)
        key = jax.random.key(seed)
        k0, k1, k2, k3 = jax.random.split(key, 4)
        hidden_states = jax.random.normal(k0, (B, S, H), dtype=jnp.float32)
        gate_w = jax.random.normal(k1, (E, H), dtype=jnp.float32) * 0.02
        gate_up_w = jax.random.normal(k2, (E, 2 * F, H), dtype=jnp.float32) * 0.02
        down_w = jax.random.normal(k3, (E, H, F), dtype=jnp.float32) * 0.02
        return {'hidden_states': hidden_states, 'gate_w': gate_w, 'gate_up_w': gate_up_w, 'down_w': down_w}
    _L0_ffn_all = _L0_ffn_setup()
    _L0_ffn_in = {k: v for k, v in _L0_ffn_all.items() if k in ('gate_w', 'gate_up_w', 'down_w')}
    del _L0_ffn_all

    def _L1_xattn_setup():
        import jax, jax.numpy as jnp
        import numpy as np
        B, S, D, H = (2, 512, 256, 16)
        DK = D // H

        def _split_heads(x):
            b, s, d = x.shape
            return x.reshape(b, s, H, DK).transpose(0, 2, 1, 3)
        key = jax.random.key(seed)
        ks = jax.random.split(key, 12)
        sc = 1.0 / np.sqrt(D)
        inp = {'q': jax.random.normal(ks[0], (B, S, D), jnp.float32), 'k': jax.random.normal(ks[1], (B, S, D), jnp.float32), 'v': jax.random.normal(ks[2], (B, S, D), jnp.float32), 'wq_w': jax.random.normal(ks[3], (D, D), jnp.float32) * sc, 'wq_b': jax.random.normal(ks[4], (D,), jnp.float32) * sc, 'wk_w': jax.random.normal(ks[5], (D, D), jnp.float32) * sc, 'wk_b': jax.random.normal(ks[6], (D,), jnp.float32) * sc, 'wv_w': jax.random.normal(ks[7], (D, D), jnp.float32) * sc, 'wv_b': jax.random.normal(ks[8], (D,), jnp.float32) * sc, 'wo_w': jax.random.normal(ks[9], (D, D), jnp.float32) * sc, 'wo_b': jax.random.normal(ks[10], (D,), jnp.float32) * sc, 'mask': jnp.tril(jnp.ones((S, S), jnp.int32))[None, None, :, :]}
        return inp
    _L1_xattn_all = _L1_xattn_setup()
    _L1_xattn_in = {k: v for k, v in _L1_xattn_all.items() if k in ('wq_w', 'wq_b', 'wk_w', 'wk_b', 'wv_w', 'wv_b', 'wo_w', 'wo_b')}
    del _L1_xattn_all

    def _L1_ffn_setup():
        import jax, jax.numpy as jnp
        import numpy as np
        B, N, D = (4, 512, 256)
        SPARSITY = 0.01
        key = jax.random.key(seed)
        k1, k2, k3 = jax.random.split(key, 3)
        x = jax.random.normal(k1, (B, N, D), dtype=jnp.float32)
        spatial = jax.random.normal(k2, (D, D), dtype=jnp.float32) * 0.02
        freq = jnp.fft.fft(spatial, axis=-1)
        k = int(D * SPARSITY)
        mag = jnp.abs(freq)
        kth = jax.lax.top_k(mag, k)[0][:, -1:]
        w_sparse = jnp.where(mag >= kth, freq, 0.0 + 0j)
        bias = jax.random.normal(k3, (D,), dtype=jnp.float32) * 0.01
        return {'x': x, 'w_freq_real': jnp.real(w_sparse).astype(jnp.float32), 'w_freq_imag': jnp.imag(w_sparse).astype(jnp.float32), 'bias': bias}
    _L1_ffn_all = _L1_ffn_setup()
    _L1_ffn_in = {k: v for k, v in _L1_ffn_all.items() if k in ('w_freq_real', 'w_freq_imag', 'bias')}
    del _L1_ffn_all
    return {'x': x, 'ctx_1024': ctx_1024, 'mask_Bx1xSxS2_if1': mask_Bx1xSxS2_if1, 'mask_1x1xSxS2_ik0': mask_1x1xSxS2_ik0, 'g_xattn': g_xattn, 'g_ffn': g_ffn, 'L0_xattn_Wq': _L0_xattn_in['Wq'], 'L0_xattn_Wk': _L0_xattn_in['Wk'], 'L0_xattn_Wv': _L0_xattn_in['Wv'], 'L0_xattn_Wo': _L0_xattn_in['Wo'], 'L0_xattn_bo': _L0_xattn_in['bo'], 'L0_ffn_gate_w': _L0_ffn_in['gate_w'], 'L0_ffn_gate_up_w': _L0_ffn_in['gate_up_w'], 'L0_ffn_down_w': _L0_ffn_in['down_w'], 'L1_xattn_wq_w': _L1_xattn_in['wq_w'], 'L1_xattn_wq_b': _L1_xattn_in['wq_b'], 'L1_xattn_wk_w': _L1_xattn_in['wk_w'], 'L1_xattn_wk_b': _L1_xattn_in['wk_b'], 'L1_xattn_wv_w': _L1_xattn_in['wv_w'], 'L1_xattn_wv_b': _L1_xattn_in['wv_b'], 'L1_xattn_wo_w': _L1_xattn_in['wo_w'], 'L1_xattn_wo_b': _L1_xattn_in['wo_b'], 'L1_ffn_w_freq_real': _L1_ffn_in['w_freq_real'], 'L1_ffn_w_freq_imag': _L1_ffn_in['w_freq_imag'], 'L1_ffn_bias': _L1_ffn_in['bias']}

def reference(x, ctx_1024, mask_Bx1xSxS2_if1, mask_1x1xSxS2_ik0, g_xattn, g_ffn, L0_xattn_Wq, L0_xattn_Wk, L0_xattn_Wv, L0_xattn_Wo, L0_xattn_bo, L0_ffn_gate_w, L0_ffn_gate_up_w, L0_ffn_down_w, L1_xattn_wq_w, L1_xattn_wq_b, L1_xattn_wk_w, L1_xattn_wk_b, L1_xattn_wv_w, L1_xattn_wv_b, L1_xattn_wo_w, L1_xattn_wo_b, L1_ffn_w_freq_real, L1_ffn_w_freq_imag, L1_ffn_bias):
    import jax
    import jax.numpy as jnp

    def _L0_xattn_ref(x, y, attention_mask, Wq, Wk, Wv, Wo, bo):
        import jax, jax.numpy as jnp
        import numpy as np
        from math import sqrt
        H = 16
        B, Sq, _ = x.shape
        Dall = Wq.shape[0]
        Dh = Dall // H
        q = (x @ Wq.T).reshape(B, Sq, H, Dh).transpose(0, 2, 1, 3)
        k = (y @ Wk.T).reshape(B, -1, H, Dh).transpose(0, 2, 1, 3)
        v = (y @ Wv.T).reshape(B, -1, H, Dh).transpose(0, 2, 1, 3)
        scores = jnp.einsum('bhqd,bhkd->bhqk', q, k)
        mask = attention_mask == 0
        scores = jnp.where(mask, jnp.float32(-1000000000.0), scores)
        attn = jax.nn.softmax(scores / sqrt(Dh), axis=-1)
        out = jnp.einsum('bhqk,bhkd->bhqd', attn, v)
        out = out.transpose(0, 2, 1, 3).reshape(B, Sq, Dall)
        return out @ Wo.T + bo

    def _L0_ffn_ref(hidden_states, gate_w, gate_up_w, down_w):
        import jax, jax.numpy as jnp
        import numpy as np
        H = 256
        F = 1024
        E = 8
        TOP_K = 2
        B, S = (1, 512)
        b, s, h = hidden_states.shape
        x = hidden_states.reshape(-1, h)
        router_logits = x @ gate_w.T
        probs = jax.nn.softmax(router_logits.astype(jnp.float32), axis=-1)
        topw, sel = jax.lax.top_k(probs, TOP_K)
        topw = topw / jnp.sum(topw, axis=-1, keepdims=True)
        topw = topw.astype(x.dtype)
        combine = jnp.sum(jax.nn.one_hot(sel, E, dtype=x.dtype) * topw[..., None], axis=1)
        gu = jnp.einsum('th,efh->etf', x, gate_up_w)
        gate, up = (gu[..., :F], gu[..., F:])
        hact = up * jax.nn.gelu(gate, approximate=False)
        expert_out = jnp.einsum('etf,ehf->eth', hact, down_w)
        out = jnp.einsum('eth,te->th', expert_out, combine)
        return out.reshape(b, s, h)

    def _L1_xattn_ref(q, k, v, wq_w, wq_b, wk_w, wk_b, wv_w, wv_b, wo_w, wo_b, mask):
        import jax, jax.numpy as jnp
        import numpy as np
        B, S, D, H = (2, 512, 256, 16)
        DK = D // H

        def _split_heads(x):
            b, s, d = x.shape
            return x.reshape(b, s, H, DK).transpose(0, 2, 1, 3)
        qh = _split_heads(q @ wq_w.T + wq_b)
        kh = _split_heads(k @ wk_w.T + wk_b)
        vh = _split_heads(v @ wv_w.T + wv_b)
        scores = jnp.einsum('bhsk,bhtk->bhst', qh, kh) / np.sqrt(DK).astype(np.float32)
        scores = jnp.where(mask == 0, jnp.float32(-1000000000.0), scores)
        probs = jax.nn.softmax(scores, axis=-1)
        attn = jnp.einsum('bhst,bhtk->bhsk', probs, vh)
        out = attn.transpose(0, 2, 1, 3).reshape(q.shape[0], q.shape[1], D)
        return out @ wo_w.T + wo_b

    def _L1_ffn_ref(x, w_freq_real, w_freq_imag, bias):
        import jax, jax.numpy as jnp
        import numpy as np
        B, N, D = (4, 512, 256)
        SPARSITY = 0.01
        w = jax.lax.complex(w_freq_real, w_freq_imag)
        x_freq = jnp.fft.fft(x, axis=-1)
        y_freq = jnp.einsum('bnd,do->bno', x_freq, w)
        y = jnp.real(jnp.fft.ifft(y_freq, axis=-1))
        return y + bias
    x = x + jnp.tanh(g_xattn[0]) * _L0_xattn_ref(_layernorm(x, axis=-1), ctx_1024, mask_Bx1xSxS2_if1, L0_xattn_Wq, L0_xattn_Wk, L0_xattn_Wv, L0_xattn_Wo, L0_xattn_bo)
    x = x + jnp.tanh(g_ffn[0]) * _L0_ffn_ref(_layernorm(x, axis=-1), L0_ffn_gate_w, L0_ffn_gate_up_w, L0_ffn_down_w)
    x = x + jnp.tanh(g_xattn[1]) * _L1_xattn_ref(_layernorm(x, axis=-1), ctx_1024, ctx_1024, L1_xattn_wq_w, L1_xattn_wq_b, L1_xattn_wk_w, L1_xattn_wk_b, L1_xattn_wv_w, L1_xattn_wv_b, L1_xattn_wo_w, L1_xattn_wo_b, mask_1x1xSxS2_ik0)
    x = x + jnp.tanh(g_ffn[1]) * _L1_ffn_ref(_layernorm(x, axis=-1), L1_ffn_w_freq_real, L1_ffn_w_freq_imag, L1_ffn_bias)
    return x

_drawn_inputs = setup_inputs


def setup_inputs(seed=0):
    import zlib

    import numpy as np

    out = dict(_drawn_inputs(seed))
    spreads = {'g_ffn': (-1.0, 0.57), 'L0_xattn_bo': (0.0, 0.1)}
    factors = {'L0_xattn_Wq': 8.0,
     'L0_xattn_Wk': 8.0,
     'L0_ffn_gate_w': 4.039,
     'L0_ffn_gate_up_w': 3.519,
     'L0_ffn_down_w': 3.522,
     'L1_xattn_wq_b': 3.907,
     'L1_xattn_wk_b': 64.0,
     'L1_ffn_bias': 8.0}
    for name, (base, spread) in spreads.items():
        noise = np.random.default_rng([zlib.crc32(name.encode()), seed]).standard_normal(out[name].shape)
        drawn = base * np.exp(spread * noise) if base else spread * noise
        out[name] = jnp.asarray(drawn.astype(out[name].dtype))
    for name, factor in factors.items():
        out[name] = (out[name] * factor).astype(out[name].dtype)
    return out
```

```python
from contextlib import ExitStack

import numpy as np

import concourse.bass as bass
from concourse import mybir

F32 = mybir.dt.float32
F16 = mybir.dt.float16
BF16 = mybir.dt.bfloat16
I32 = mybir.dt.int32
U32 = mybir.dt.uint32
ALU = mybir.AluOpType
ACT = mybir.ActivationFunctionType
AX = mybir.AxisListType.X

P = 128
NB, S, D = 16, 256, 256
S2 = 77
H, DH = 16, 16
KC = D // P
QT = S // P
HC = H // KC
E, F = 8, 1024
FC = F // P
TILES = 2 * NB + E
CAP = NB * S + S
SCALE = 64.0
INV = 1.0 / SCALE
BIG = 2.0 ** 100
EPS = 1e-5
ROOT = 0.25
MROW = 96
MK = MROW + H
GP = 2 * H // 4
NW = 8
PASSES = ((0, 0), (0, 1), (1, 0))

C_ID, C_UT, C_ONE, C_SEL, C_IOTA, C_BASE, C_MH = 0, 128, 256, 384, 392, 400, 408
C_END = C_MH + H * S2


class Batch:

    def __init__(self, layer, i, half, par):
        self.i, self.par = i, par
        self.n = i + NB * layer
        self.half = half + NB // 2 * layer
        self.own = half
        self.layer, self._half = layer, half

    def after(self, k):
        up = (self.par + k) // 2
        return Batch(self.layer, self.i + k, self._half + up, (self.par + k) % 2)


def at(layer, i):
    return Batch(layer, i, i // 2, i % 2)


def steps(eng, layer, step):
    step(at(layer, 0), True, False, True, True)
    step(at(layer, 1), True, True, True, True)
    step(at(layer, 2), True, True, True, True)
    with eng.Fori(0, 5) as j:
        step(Batch(layer, j * 2 + 3, j + 1, 1), True, True, True, True)
        step(Batch(layer, j * 2 + 4, j + 2, 0), True, True, True, True)
    step(at(layer, 13), True, True, True, False)
    step(at(layer, 14), True, True, False, False)
    step(at(layer, 15), False, True, False, False)


class Signals:
    pass


class Chain:

    def __init__(self, eng, sem, per, i, wait=None):
        self.eng, self.sem, self.per, self.i, self.k = eng, sem, per, i, 0
        self.wait = wait or type(eng).wait_ge

    def link(self, ins):
        self.k += 1
        assert self.k <= self.per, self.sem
        ins.then_inc(self.sem, 1)
        self.wait(self.eng, self.sem, self.i * self.per + self.k)

    def end(self):
        assert self.k == self.per, (self.k, self.per)


def build(nc, a, out):
    x_d = a["x"].rearrange("b s d -> (b s) d")
    out_d = out.rearrange("b s d -> (b s) d")
    m0_d = a["mask0"].rearrange("b o s k -> (b o s) k")
    m1_d = a["mask1"].rearrange("b o s k -> (b o s) k")
    x1_d = nc.dram_tensor("x1_scratch", (NB * S, D), F32, kind="Internal").ap()
    xs_d = nc.dram_tensor("expert_in", (E * CAP, D), F32, kind="Internal").ap()
    ys_d = nc.dram_tensor("expert_out", (TILES * S, D), F32, kind="Internal").ap()

    def rows(dram, start):
        return dram[bass.ds(start, S), :].rearrange("(p t) d -> p t d", t=QT)

    def tile_row(e, g, t0):
        return nc.s_assert_within(e * CAP + g * S - t0 * S, 0, E * CAP - S,
                                  skip_runtime_bounds_check_because="an expert has at most NB * S rows")

    with ExitStack() as ctx:
        def sb(name, shape, dt):
            return ctx.enter_context(nc.sbuf_tensor(name, shape, dt))

        def sem(name):
            return ctx.enter_context(nc.semaphore(name))

        bank = [ctx.enter_context(nc.psum_tensor(f"bank{i}", [P, 512], F32)) for i in range(8)]
        b_t, b_proj, b_small = bank[0], bank[1], bank[2]
        b_s, b_top, b_pv = bank[3:5], bank[5], bank[6:8]
        b_f = bank[3:6]

        cst = sb("cst", [P, C_END], F32)
        ident = cst[:, C_ID:C_ID + P]
        identb = sb("identb", [P, P], BF16)
        utb = sb("utb", [P, P], BF16)
        oneb = sb("oneb", [P, P], BF16)
        mhead = sb("mhead", [MK, H, S2], BF16)
        mhalf = sb("mhalf", [P, QT], F32)
        cell = sb("cell", [1, 130], F32)
        gates = sb("gates", [P, 4], F32)
        tg = sb("tg", [P, 4], F32)
        tgs = sb("tgs", [P, 4], F32)
        we_flat = sb("we", [P, 2, 3 * 2 * 2048], F16)
        we = we_flat[:].rearrange("p b (k i n) -> p b k i n", k=3, i=2)
        early = we_flat[:, 1].bitcast(F32)
        wst = early[:, 0:NW * KC * D].rearrange("p (k n) -> p k n", k=NW)
        wf = early[:, 4096:5120].rearrange("p (k c n) -> p k c n", k=2, c=KC)
        afT = early[:, 5120:6144].rearrange("p (k c n) -> p k c n", k=2, c=KC)
        wat = sb("wat", [P, NW, 2, KC, D], F16)
        ctxs = sb("ctxs", [P, 2, KC, NB * S2], F16)
        bias = sb("bias", [P, 4, D], F32)
        bkq = sb("bkq", [P, KC], F32)
        bqrow = sb("bqrow", [P, D], F32)
        bqz = sb("bqz", [P, 2, D], F16)
        nfT = sb("nfT", [P, S], BF16)
        dft = sb("dft", [P, 3, KC, D], F32)
        mf = sb("mf", [P, 2, KC, D], F16)
        xin = sb("xin", [P, 2, QT, D], F32)
        mraw = sb("mraw", [P, 2, QT, S2], I32)
        xb = sb("xb", [P, 2, QT, D], F32)
        eqf = sb("eqf", [P, QT, S2], F32)
        full = sb("full", [P, QT], F32)
        nf = sb("nf", [P, QT], F32)
        nfb = sb("nfb", [P, QT], BF16)
        nbig = sb("nbig", [P, QT], F32)
        bm = sb("bm", [P, QT, MK], BF16)
        st = sb("st", [P, 2, QT, 6], F32)
        mv = sb("mv", [P, 2, QT, 2], F32)
        ve = sb("ve", [P, 2, QT], F32)
        rstd = sb("rstd", [P, 2, QT], F32)
        rq = sb("rq", [P, QT], F32)
        h = sb("h", [P, QT, D], F32)
        hT = sb("hT", [P, 2, KC, S], F16)
        qT = sb("qT", [P, 2, 2, KC, S], F16)
        kf = sb("kf", [P, KC, S2], F32)
        kp = sb("kp", [P, 2, KC, S2], F16)
        kbd = sb("kbd", [P, 2, 2, KC, HC, S2], F16)
        vaug = sb("vaug", [P, 2, H, DH + 1], F32)
        mrhs = sb("mrhs", [MK, S], BF16)
        pr = sb("pr", [P, 4, 2 * S], F32)
        rden = sb("rden", [P, QT, H], F32)
        att = sb("att", [P, QT, D], F32)
        aT = sb("aT", [P, 2, KC, S], F16)
        x1 = sb("x1", [P, 2, QT, D], F32)
        x3b = sb("x3b", [P, 2, QT, D], F32)
        h2 = sb("h2", [P, 2, QT, D], F32)
        h2T = sb("h2T", [P, KC, S], F32)
        h2s = sb("h2s", [P, 2, KC, S], F16)
        ob = sb("ob", [P, 2, QT, D], F32)
        wg = sb("wg", [P, KC, E], F32)
        lg = sb("lg", [P, QT, E], F32)
        top = sb("top", [P, QT, 8], F32)
        topi = sb("topi", [P, QT, 8], U32)
        topf = sb("topf", [P, QT, 8], F32)
        oh = sb("oh", [P, QT, 2, E], F32)
        pick = sb("pick", [P, QT, E], BF16)
        carry = sb("carry", [P, E], F32)
        rank = sb("rank", [P, QT, E], F32)
        sel2 = sb("sel2", [P, QT, 2, E], F32)
        slotf = sb("slotf", [P, QT, 2], F32)
        slot = sb("slot", [P, 2, QT * 2], I32)
        slots = sb("slots", [P, NB, QT * 2], I32)
        gap = sb("gap", [P, NB, QT], F32)
        wexp = sb("wexp", [P, NB, QT], F32)
        wone = sb("wone", [P, NB, QT], F32)
        wtok = sb("wtok", [P, NB, QT, 2], F32)
        wcur = sb("wcur", [P, 2, QT * 2], F32)
        yg = sb("yg", [P, 2, QT, 2, D], F32)
        nti = sb("nti", [P, E], I32)
        nti2 = sb("nti2", [P, E], I32)
        ntf = sb("ntf", [P, E], F32)
        tsf = sb("tsf", [P, E + 1], F32)
        shift = sb("shift", [P, E], F32)
        slotx = sb("slotx", [P, NB * QT * 2], F32)
        slott = sb("slott", [P, NB * QT * 2], F32)
        slotz = sb("slotz", [P, NB * QT * 2], F32)
        tbl = sb("tbl", [1, 2 * E + 1], I32)
        zeros = sb("zeros", [P, QT, D], F32)
        wes = sb("wes", [P, 1, 2048], F32)
        tiles = sb("tiles", [P, 3584], F32)
        xs = tiles[:, 0:512].rearrange("p (t n) -> p t n", t=QT)
        ysb = tiles[:, 512:1024].rearrange("p (t n) -> p t n", t=QT)
        xT = tiles[:, 1024:1536].bitcast(F16).rearrange("p (i c n) -> p i c n", i=2, c=KC)
        ge = tiles[:, 1536:2048].rearrange("p (b n) -> p b n", b=2)
        a32 = tiles[:, 2048:2560].rearrange("p (b n) -> p b n", b=2)
        act16 = tiles[:, 2560:3584].bitcast(F16).rearrange("p (b i n) -> p b i n", b=4, i=2)
        ctx32 = tiles[:, 0:KC * NB * S2].rearrange("p (c n) -> p c n", c=KC)

        s = Signals()
        s.consts_in = sem("consts_in")
        s.context_in = sem("context_in")
        s.attention_weights_in = sem("attention_weights_in")
        s.fourier_in = sem("fourier_in")
        s.small_inputs_in = sem("small_inputs_in")
        s.pool_setup = sem("pool_setup")
        s.dve_setup = sem("dve_setup")
        s.act_setup = sem("act_setup")
        s.fourier_product = sem("fourier_product")
        s.fourier_read = sem("fourier_read")
        s.unmasked_turned = sem("unmasked_turned")
        s.unmasked_ready = sem("unmasked_ready")
        s.rows_in_even = sem("rows_in_even")
        s.rows_in_odd = sem("rows_in_odd")
        s.variance = sem("variance")
        s.root = sem("root")
        s.variance_after = sem("variance_after")
        s.root_after = sem("root_after")
        s.residual_base = sem("residual_base")
        s.normed = sem("normed")
        s.normed_turned = sem("normed_turned")
        s.normed_high = sem("normed_high")
        s.normed_low = sem("normed_low")
        s.queries = sem("queries")
        s.queries_high = sem("queries_high")
        s.queries_low = sem("queries_low")
        s.keys_values = sem("keys_values")
        s.keys_out = sem("keys_out")
        s.values_out = sem("values_out")
        s.keys_split = sem("keys_split")
        s.keys_diagonal = sem("keys_diagonal")
        s.top_scores = sem("top_scores")
        s.maxima = sem("maxima")
        s.mask_turned = sem("mask_turned")
        s.mask_ready = sem("mask_ready")
        s.scores = sem("scores")
        s.weights = sem("weights")
        s.weighted_values = sem("weighted_values")
        s.attended = sem("attended")
        s.attended_turned = sem("attended_turned")
        s.attended_high = sem("attended_high")
        s.attended_low = sem("attended_low")
        s.attention_out = sem("attention_out")
        s.row_update = sem("row_update")
        s.update_stored_even = sem("update_stored_even")
        s.update_stored_odd = sem("update_stored_odd")
        s.normed_after = sem("normed_after")
        s.normed_after_turned = sem("normed_after_turned")
        s.normed_after_high = sem("normed_after_high")
        s.normed_after_low = sem("normed_after_low")
        s.table_zeroed = sem("table_zeroed")
        s.logits = sem("logits")
        s.picked = sem("picked")
        s.prefix = sem("prefix")
        s.placed = sem("placed")
        s.scattered_even = sem("scattered_even")
        s.scattered_odd = sem("scattered_odd")
        s.fourier_out = sem("fourier_out")
        s.final_base = sem("final_base")
        s.final_rows = sem("final_rows")
        s.final_stored_even = sem("final_stored_even")
        s.final_stored_odd = sem("final_stored_odd")
        s.gathered_even = sem("gathered_even")
        s.gathered_odd = sem("gathered_odd")
        s.experts_added = sem("experts_added")
        s.route_step = sem("route_step")
        s.place_step = sem("place_step")
        s.token_weights = sem("token_weights")
        s.mask_step = sem("mask_step")
        s.norm_step = sem("norm_step")
        s.attended_step = sem("attended_step")
        s.stats_step = sem("stats_step")
        s.stats_after_step = sem("stats_after_step")
        s.root_step = sem("root_step")
        s.root_after_step = sem("root_after_step")
        s.combine_step = sem("combine_step")
        s.places_recalled = sem("places_recalled")
        s.padding_zeroed = sem("padding_zeroed")
        s.tiles_counted = sem("tiles_counted")
        s.gap_exponential = sem("gap_exponential")
        s.expert_weights_in = sem("expert_weights_in")
        s.expert_weights = sem("expert_weights")
        s.split_step = sem("split_step")
        s.tile_turned = sem("tile_turned")
        s.tile_in = sem("tile_in")
        s.tile_high = sem("tile_high")
        s.tile_low = sem("tile_low")
        s.gate_up = sem("gate_up")
        s.gelu = sem("gelu")
        s.product = sem("product")
        s.activation = sem("activation")
        s.down = sem("down")
        s.expert_rows = sem("expert_rows")
        s.expert_rows_stored = sem("expert_rows_stored")
        s.credits_given = sem("credits_given")
        s.count_step = sem("count_step")

        used = []

        def wait_apart(eng, which, value):
            eng.wait_ge(which, value)
            if not isinstance(value, int):
                used.append(1)
                n = 2 + len(used) % 128
                if eng is nc.vector:
                    eng.memset(cell[0:1, n:n + 1], 0.0)
                else:
                    eng.tensor_tensor(cell[0:1, n:n + 1], cell[0:1, 1:2], cell[0:1, 1:2], ALU.add)

        s_scat = (s.scattered_even, s.scattered_odd)
        s_gat = (s.gathered_even, s.gathered_odd)
        s_xin = (s.rows_in_even, s.rows_in_odd)
        s_x1st = (s.update_stored_even, s.update_stored_odd)
        s_ost = (s.final_stored_even, s.final_stored_odd)
        block = ctx.enter_context(nc.Block())

        @block.sync
        def _(sp):
            def load(b):
                src = (x_d, x1_d)[b.layer]
                sp.dma_start(xin[:, b.par], rows(src, b.i * S)).then_inc(s_xin[b.par], 16)
                msk = rows(m0_d, b.i * S) if b.layer == 0 else rows(m1_d, 0)
                sp.dma_start(mraw[:, b.par], msk).then_inc(s_xin[b.par], 16)

            load(at(0, 0))
            sp.dma_start(cst[:], a["consts"]).then_inc(s.consts_in, 16)
            sp.dma_start(ctx32, a["ctxT"].rearrange("(c p) n -> p c n", p=P)).then_inc(s.context_in, 16)
            for k in range(NW):
                sp.dma_start(wst[:, k].rearrange("p (c n) -> p c n", c=KC),
                             a[f"w{k}"].rearrange("(c p) n -> p c n", p=P)).then_inc(s.attention_weights_in, 16)
            sp.dma_start(gates[:], a["gates"].partition_broadcast(P)).then_inc(s.small_inputs_in, 16)
            for k, name in enumerate(("bo0", "bo1", "fb", "bv")):
                sp.dma_start(bias[:, k], a[name].partition_broadcast(P)).then_inc(s.small_inputs_in, 16)
            sp.dma_start(bkq[:], a["bk"]).then_inc(s.small_inputs_in, 16)
            sp.dma_start(bqrow[0:1, :], a["bq"].rearrange("(o d) -> o d", o=1)).then_inc(s.small_inputs_in, 16)
            sp.dma_start(wg[:], a["gwT"].rearrange("(c p) e -> p c e", p=P)).then_inc(s.small_inputs_in, 16)
            load(at(0, 1))
            for k, name in enumerate(("dcos", "dsin", "dnsin")):
                sp.dma_start(dft[:, k], a[name].rearrange("(c p) n -> p c n", p=P)).then_inc(s.fourier_in, 16)
            for k, name in enumerate(("wfr", "wfi")):
                sp.dma_start(wf[:, k], a[name].rearrange("(c p) n -> p c n", p=P)).then_inc(s.fourier_in, 16)

            def free_and_load(b):
                sp.wait_ge(s.normed, b.n - 1)
                sp.wait_ge(s.residual_base, b.n - 1)
                load(b)

            def step0(b, front, tail, pre, ld):
                if ld:
                    free_and_load(b.after(3))
                if tail:
                    keep(b.after(-1))

            def keep(b):
                sp.wait_ge(s.row_update, b.n + 1)
                sp.dma_start(rows(x1_d, b.i * S), x1[:, b.par]).then_inc(s_x1st[b.par], 16)

            free_and_load(at(0, 2))
            sp.wait_ge(s.pool_setup, 7)
            for k in range(5):
                n = TILES * S // P // 5
                dst = ys_d.rearrange("(k p t) d -> k p t d", k=5, p=P)[k]
                sp.dma_start(dst, zeros[:, 0:1].to_broadcast([P, n, D])).then_inc(s.table_zeroed, 16)
            steps(sp, 0, step0)
            keep(at(0, 15))

            for k in range(2):
                sp.wait_ge(s_x1st[k], 16 * (NB // 2))
            sp.wait_ge(s.tiles_counted, 1)
            for k in range(2):
                sp.wait_ge(s_scat[k], 64 * (NB // 2))
            sp.wait_ge(s.padding_zeroed, 16 * E)
            with sp.Fori(0, E) as e:
                t0 = sp.value_load(tbl[0:1, bass.ds(e, 1)], min_val=0, max_val=TILES)
                t1 = sp.value_load(tbl[0:1, bass.ds(e + 1, 1)], min_val=1, max_val=TILES)
                with sp.Fori(t0, t1) as g:
                    sp.wait_ge(s.tile_turned, g + 1)
                    row = tile_row(e, g, t0)
                    sp.dma_start(xs, rows(xs_d, row)).then_inc(s.tile_in, 16)
            tend = sp.value_load(tbl[0:1, E:E + 1], min_val=1, max_val=TILES)
            sp.wait_ge(s.tile_turned, tend + 1)
            sp.dma_start(xs, rows(xs_d, 0)).then_inc(s.tile_in, 16)

            def step1(b, front, tail, pre, ld):
                if ld:
                    free_and_load(b.after(3))
                if tail:
                    store(b.after(-1))

            def store(b):
                sp.wait_ge(s.final_rows, b.i + 1)
                sp.dma_start(rows(out_d, b.i * S), ob[:, b.par]).then_inc(s_ost[b.par], 16)

            for i in range(3):
                free_and_load(at(1, i))
            steps(sp, 1, step1)
            store(at(1, 15))
            for k in range(2):
                sp.wait_ge(s_ost[k], 16 * (NB // 2))

        @block.gpsimd
        def _(pool):
            def weights(chunk, part, par, waited=None):
                ch = Chain(pool, s.split_step, 2, chunk, wait_apart)
                stage = wes[:, 0]
                ch.link(pool.tensor_scalar(stage, stage, SCALE, 1.0, ALU.mult, ALU.mult))
                ch.link(pool.tensor_copy(we[:, par, part, 0], stage))
                pool.tensor_tensor(we[:, par, part, 1], stage, we[:, par, part, 0],
                                   ALU.subtract).then_inc(s.expert_weights, 1)

            def fetch(expert, part):
                if part < 2:
                    src = a["guT"][bass.ds(expert * D + part * P, P), :]
                else:
                    src = a["dnT"][bass.ds(expert * F, F), :].rearrange("(c p) n -> p c n", p=P)
                dst = wes[:, 0] if part < 2 else wes[:, 0].rearrange("p (c n) -> p c n", c=FC)
                pool.dma_start(dst, src).then_inc(s.expert_weights_in, 16)

            def ln_root(kind, count, done, b):
                ch = Chain(pool, (s.root_step, s.root_after_step)[kind], 1, b.n)
                wait_apart(pool, done, b.n + 1)
                ch.link(pool.tensor_scalar(ve[:, kind], mv[:, kind, :, 1], EPS, 1.0, ALU.add, ALU.mult))
                pool.tensor_tensor(rstd[:, kind], ve[:, kind], mhalf[:], ALU.pow).then_inc(count, 1)

            def base(b):
                pool.wait_ge(s_xin[b.par], 32 * (b.half + 1))
                if b.layer == 1:
                    pool.wait_ge(s.experts_added, b.i + 1)
                if not (isinstance(b.n, int) and b.n < 2):
                    pool.wait_ge(s.row_update, b.n - 1)
                pool.tensor_tensor(xb[:, b.par], xin[:, b.par],
                                   bias[:, b.layer].unsqueeze(1).to_broadcast([P, QT, D]),
                                   ALU.add).then_inc(s.residual_base, 1)

            def root(b):
                ln_root(0, s.root, s.variance, b)

            def kdiag(b):
                wait_apart(pool, s.keys_out, b.n + 1)
                if not (isinstance(b.n, int) and b.n < 1):
                    wait_apart(pool, s.keys_diagonal, 2 * b.n)
                pool.tensor_copy(kp[:, 0], kf[:]).then_inc(s.keys_split, 1)
                pool.wait_ge(s.keys_split, 2 * b.n + 1)
                pool.tensor_tensor(kp[:, 1], kf[:], kp[:, 0], ALU.subtract).then_inc(s.keys_split, 1)
                pool.wait_ge(s.keys_split, 2 * b.n + 2)
                if not (isinstance(b.n, int) and b.n < 2):
                    pool.wait_ge(s.scores, GP * (b.n - 1))
                for k in range(2):
                    for c in range(KC):
                        ins = pool.tensor_tensor(
                            kbd[:, b.par, k, c],
                            kp[:, k, c].unsqueeze(1).to_broadcast([P, HC, S2]),
                            cst[:, C_SEL:C_SEL + HC].unsqueeze(2).to_broadcast([P, HC, S2]), ALU.mult)
                    ins.then_inc(s.keys_diagonal, 1)

            def scatter(b):
                wait_apart(pool, s.placed, b.i + 1)
                for t in range(QT):
                    for k in range(2):
                        pool.indirect_dma_start(
                            out=xs_d, out_offset=bass.IndirectOffsetOnAxis(
                                ap=slot[:, b.par, 2 * t + k:2 * t + k + 1], axis=0),
                            in_=h2[:, b.par, t], in_offset=None).then_inc(s_scat[b.par], 16)

            def gather(b):
                wait_apart(pool, s.places_recalled, b.i + 1)
                for t in range(QT):
                    for k in range(2):
                        pool.indirect_dma_start(
                            out=yg[:, b.par, t, k], out_offset=None, in_=ys_d,
                            in_offset=bass.IndirectOffsetOnAxis(
                                ap=slot[:, b.par, 2 * t + k:2 * t + k + 1], axis=0)).then_inc(s_gat[b.par], 16)

            def residual3(b):
                pool.wait_ge(s.row_update, b.n + 1)
                if not (isinstance(b.i, int) and b.i < 2):
                    pool.wait_ge(s.final_rows, b.i - 1)
                pool.tensor_tensor(x3b[:, b.par], x1[:, b.par],
                                   bias[:, 2].unsqueeze(1).to_broadcast([P, QT, D]),
                                   ALU.add).then_inc(s.final_base, 1)

            def step(b, front, tail, pre, ld):
                pv = b.after(-1)
                if front:
                    base(b.after(1))
                if tail:
                    ln_root(1, s.root_after, s.variance_after, pv)
                if pre:
                    root(b.after(2))
                if tail and b.layer == 1:
                    residual3(pv)
                if tail and b.layer == 0:
                    scatter(pv)
                if ld and b.layer == 1:
                    gather(b.after(3))
                if pre:
                    kdiag(b.after(2))
                if b.layer == 0 and isinstance(b.i, int) and b.i in (13, 14):
                    part = b.i - 12
                    pool.wait_ge(s.expert_weights, part)
                    fetch(0, part)
                    pool.wait_ge(s.expert_weights_in, 16 * (part + 1))
                    weights(part, part, 0)

            pool.memset(cell[0:1, 1:2], 0.0).then_inc(s.pool_setup, 1)
            pool.memset(mhalf[:], -0.5).then_inc(s.pool_setup, 1)
            pool.memset(zeros[:], 0.0).then_inc(s.pool_setup, 1)
            pool.memset(bm[:], 0.0).then_inc(s.pool_setup, 1)
            pool.memset(nfT[:], 0.0).then_inc(s.pool_setup, 1)
            pool.memset(bqz[:], 0.0).then_inc(s.pool_setup, 1)
            pool.memset(vaug[:], 1.0).then_inc(s.pool_setup, 1)
            pool.wait_ge(s.pool_setup, 7)
            pool.wait_ge(s.consts_in, 16)
            pool.wait_ge(s.dve_setup, 3)
            root(at(0, 0))
            kdiag(at(0, 0))
            base(at(0, 0))
            kdiag(at(0, 1))
            root(at(0, 1))
            fetch(0, 0)
            pool.wait_ge(s.expert_weights_in, 16)
            weights(0, 0, 0)
            steps(pool, 0, step)
            ln_root(1, s.root_after, s.variance_after, at(0, 15))
            scatter(at(0, 15))

            pool.wait_ge(s.tiles_counted, 1)
            with pool.Fori(0, E) as e:
                end = pool.value_load(tbl[0:1, bass.ds(e + (E + 1), 1)], min_val=0, max_val=E * CAP - S)
                pool.dma_start(rows(xs_d, end), zeros[:]).then_inc(s.padding_zeroed, 16)

            def expert(e, par, first=False):
                for part in range(3):
                    chunk = e * 3 + part
                    pool.wait_ge(s.expert_weights, chunk)
                    if not first and part == 0:
                        gone = pool.value_load(tbl[0:1, bass.ds(e - 1, 1)], min_val=1, max_val=TILES)
                        pool.wait_ge(s.down, gone * FC + FC)
                    fetch(e, part)
                    wait_apart(pool, s.expert_weights_in, (chunk + 1) * 16)
                    weights(chunk, part, par)

            expert(1, 1, True)
            with pool.Fori(1, E // 2) as pair:
                expert(pair * 2, 0)
                expert(pair * 2 + 1, 1)

            tend = pool.value_load(tbl[0:1, E:E + 1], min_val=1, max_val=TILES)
            wait_apart(pool, s.expert_rows_stored, (tend + 1) * 16)
            gather(at(1, 0))
            gather(at(1, 1))
            root(at(1, 0))
            kdiag(at(1, 0))
            base(at(1, 0))
            gather(at(1, 2))
            kdiag(at(1, 1))
            root(at(1, 1))
            steps(pool, 1, step)
            ln_root(1, s.root_after, s.variance_after, at(1, 15))
            residual3(at(1, 15))

        @block.scalar
        def _(act):
            def h_hi(b):
                act.wait_ge(s.normed_turned, b.n + 1)
                act.activation(hT[:, 0], b_t[:].rearrange("p (c n) -> p c n", c=KC),
                               ACT.Copy).then_inc(s.normed_high, 1)

            def q_hi(b):
                act.wait_ge(s.queries, b.n + 1)
                if not (isinstance(b.n, int) and b.n < 2):
                    act.wait_ge(s.scores, GP * (b.n - 1))
                act.activation(qT[:, b.par, 0], b_proj[:].rearrange("p (c n) -> p c n", c=KC),
                               ACT.Copy, scale=INV).then_inc(s.queries_high, 1)

            def k_out(b):
                act.wait_ge(s.keys_values, b.n + 1)
                if not (isinstance(b.n, int) and b.n < 1):
                    act.wait_ge(s.keys_split, 2 * b.n)
                for c in range(KC):
                    ins = act.activation(kf[:, c], b_small[:, c * S2:(c + 1) * S2], ACT.Identity,
                                         bias=bkq[:, c:c + 1] if b.layer else 0.0, scale=INV)
                ins.then_inc(s.keys_out, 1)

            def m_out(b):
                act.wait_ge(s.mask_turned, b.n + 1)
                act.activation(mrhs[:], b_top[0:MK, 384:512].bitcast(BF16), ACT.Copy).then_inc(s.mask_ready, 1)

            def expo(b, g):
                act.wait_ge(s.scores, b.n * GP + g + 1)
                if not (isinstance(b.n, int) and b.n * GP + g < 4):
                    act.wait_ge(s.weighted_values, b.n * GP + (g - 3))
                act.activation(pr[0:S2, g % 4], b_s[g % 2][0:S2, :], ACT.Exp,
                               scale=ROOT).then_inc(s.weights, 1)

            def tail_out(b):
                act.wait_ge(s.normed_after_turned, b.n + 1)
                src = b_t[:].rearrange("p (c n) -> p c n", c=KC)
                dst = h2T[:] if b.layer == 0 else h2s[:, 0]
                act.activation(dst, src, ACT.Copy).then_inc(s.normed_after_high, 1)

            def a_hi(b):
                act.wait_ge(s.attended_turned, b.n + 1)
                act.activation(aT[:, 0], b_t[:].rearrange("p (c n) -> p c n", c=KC),
                               ACT.Copy).then_inc(s.attended_high, 1)

            def step(b, front, tail, pre, ld):
                nx, pv = b.after(1), b.after(-1)
                expo(b, 0)
                expo(b, 1)
                expo(b, 2)
                if front:
                    h_hi(nx)
                expo(b, 3)
                if front:
                    q_hi(nx)
                expo(b, 4)
                if tail:
                    tail_out(pv)
                expo(b, 5)
                expo(b, 6)
                expo(b, 7)
                if pre:
                    k_out(b.after(2))
                if front:
                    m_out(nx)
                a_hi(b)

            act.wait_ge(s.small_inputs_in, 16 * 8)
            act.activation(tg[:], gates[:], ACT.Tanh).then_inc(s.act_setup, 1)
            for k in range(NW):
                if k == 0:
                    act.wait_ge(s.attention_weights_in, 16 * NW)
                act.activation(wat[:, k, 0].rearrange("p c n -> p (c n)"), wst[:, k], ACT.Copy,
                               scale=SCALE).then_inc(s.act_setup, 1)
            act.wait_ge(s.context_in, 16)
            act.activation(ctxs[:, 0], ctx32, ACT.Copy).then_inc(s.act_setup, 1)
            act.wait_ge(s.pool_setup, 6)
            act.activation(bqz[0:1, 0], bqrow[0:1, :], ACT.Copy, scale=SCALE).then_inc(s.act_setup, 1)
            for k in range(2):
                act.wait_ge(s.fourier_product, k + 1)
                act.activation(afT[:, k], b_f[k][:].rearrange("p (c n) -> p c n", c=KC),
                               ACT.Copy).then_inc(s.fourier_read, 1)
            act.wait_ge(s.fourier_product, 3)
            act.activation(mf[:, 0], b_f[2][:].rearrange("p (c n) -> p c n", c=KC), ACT.Copy,
                           scale=SCALE / D).then_inc(s.fourier_read, 1)
            h_hi(at(0, 0))
            k_out(at(0, 0))
            q_hi(at(0, 0))
            k_out(at(0, 1))
            m_out(at(0, 0))
            steps(act, 0, step)
            tail_out(at(0, 15))
            act.wait_ge(s.gap_exponential, 1)
            act.activation(wexp[:], gap[:], ACT.Exp).then_inc(s.gap_exponential, 1)

            act.wait_ge(s.tiles_counted, 1)

            def x_hi(g):
                act.wait_ge(s.tile_turned, g + 2)
                act.activation(xT[:, 0], b_t[:].rearrange("p (c n) -> p c n", c=KC),
                               ACT.Copy).then_inc(s.tile_high, 1)

            act.wait_ge(s.credits_given, 1)
            act.wait_ge(s.table_zeroed, 16 * 5)
            x_hi(0)
            with act.Fori(0, E) as e:
                t0 = act.value_load(tbl[0:1, bass.ds(e, 1)], min_val=0, max_val=TILES)
                t1 = act.value_load(tbl[0:1, bass.ds(e + 1, 1)], min_val=1, max_val=TILES)
                with act.Fori(t0, t1) as g:
                    for fc in range(FC):
                        act.wait_ge(s.gate_up, g * FC + (fc + 1))
                        act.wait_ge(s.product, g * FC + (fc + 7))
                        act.activation(ge[:, fc % 2], bank[1 + fc % 3][:, 0:S], ACT.Gelu,
                                       scale=INV).then_inc(s.gelu, 1)
                    x_hi(g + 1)
                    act.wait_ge(s.down, g * FC + 2 * FC)
                    act.wait_ge(s.expert_rows_stored, g * 16 + 16)
                    for t in range(QT):
                        act.activation(ysb[:, t], bank[4 + t][:, 0:D], ACT.Copy,
                                       scale=INV).then_inc(s.expert_rows, 1)
                    act.wait_ge(s.expert_rows, g * 2 + 4)
                    act.dma_start(rows(ys_d, g * S), ysb).then_inc(s.expert_rows_stored, 16)

            h_hi(at(1, 0))
            act.wait_ge(s.unmasked_turned, 1)
            act.activation(nfT[0:1, :], b_top[0:1, 384:512].bitcast(BF16), ACT.Copy).then_inc(s.unmasked_ready, 1)
            k_out(at(1, 0))
            q_hi(at(1, 0))
            k_out(at(1, 1))
            m_out(at(1, 0))
            steps(act, 1, step)
            tail_out(at(1, 15))

        @block.vector
        def _(dve):
            def stats(kind, src, sem_done, b, par):
                ch = Chain(dve, (s.stats_step, s.stats_after_step)[kind], 1, b.n, wait_apart)
                dve.bn_stats(st[:, kind, 0], src[:, par, 0])
                ch.link(dve.bn_stats(st[:, kind, 1], src[:, par, 1]))
                dve.bn_aggr(mv[:, kind, 0], st[:, kind, 0])
                dve.bn_aggr(mv[:, kind, 1], st[:, kind, 1]).then_inc(sem_done, 1)

            def pre_stats(b):
                dve.wait_ge(s_xin[b.par], 32 * (b.half + 1))
                if b.layer == 1:
                    dve.wait_ge(s_gat[b.par], b.own * 64 + 64)
                    dve.tensor_copy(wcur[:, b.par], wtok[:, bass.ds(b.i, 1)].rearrange(
                        "p o t k -> p (o t k)")).then_inc(s.combine_step, 1)
                    dve.wait_ge(s.combine_step, b.i * 3 + 1)
                    for k in range(2):
                        for t in range(QT):
                            ins = dve.scalar_tensor_tensor(
                                xin[:, b.par, t], yg[:, b.par, t, k],
                                wcur[:, b.par, 2 * t + k:2 * t + k + 1], xin[:, b.par, t],
                                ALU.mult, ALU.add)
                        ins.then_inc(s.combine_step, 1)
                        dve.wait_ge(s.combine_step, b.i * 3 + k + 2)
                stats(0, xin, s.variance, b, b.par)
                if b.layer == 1:
                    dve.tensor_copy(zeros[:, 0, 0:1], wcur[:, b.par, 0:1]).then_inc(s.experts_added, 1)

            def mask_rows(b, first=False):
                if not first:
                    dve.wait_ge(s.mask_turned, b.n)
                ch = Chain(dve, s.mask_step, 3, b.n)
                ch.link(dve.tensor_scalar(eqf[:], mraw[:, b.par], 0, None, ALU.is_equal))
                ch.link(dve.tensor_reduce(full[:], eqf[:], AX, ALU.min))
                dve.tensor_scalar(nf[:], full[:], -1.0, 1.0, ALU.mult, ALU.add)
                ch.link(dve.tensor_scalar(nbig[:], full[:], BIG, -BIG, ALU.mult, ALU.add))
                dve.tensor_tensor(bm[:, :, 0:S2], eqf[:],
                                  nbig[:].unsqueeze(2).to_broadcast([P, QT, S2]), ALU.mult)

            def pre_norm(b, first=False):
                if b.layer == 0:
                    mask_rows(b, first)
                ch = Chain(dve, s.norm_step, 1, b.n)
                dve.wait_ge(s.root, b.n + 1)
                ch.link(dve.tensor_tensor(rq[:], rstd[:, 0], nf[:], ALU.mult))
                if not first:
                    dve.wait_ge(s.normed_turned, b.n)
                for t in range(QT):
                    ins = dve.tensor_scalar(h[:, t], xin[:, b.par, t], mv[:, 0, t, 0:1], rq[:, t:t + 1],
                                            ALU.subtract, ALU.mult)
                ins.then_inc(s.normed, 1)

            def low(dst, hi, src, done, hi_done, n, scale):
                dve.wait_ge(hi_done, n + 1)
                dve.scalar_tensor_tensor(dst, src[:].rearrange("p (c n) -> p c n", c=KC), scale, hi,
                                         ALU.mult, ALU.subtract).then_inc(done, 1)

            def v_out(b):
                dve.wait_ge(s.keys_out, b.n + 1)
                if not (isinstance(b.n, int) and b.n < 2):
                    dve.wait_ge(s.weighted_values, GP * (b.n - 1))
                dst = vaug[0:S2, b.par, :, 0:DH]
                src = b_small[0:S2, 160:416].rearrange("p (h d) -> p h d", h=H)
                if b.layer == 0:
                    dve.tensor_scalar(dst, src, INV, None, ALU.mult).then_inc(s.values_out, 1)
                else:
                    dve.scalar_tensor_tensor(dst, src, INV,
                                             bias[0:S2, 3].rearrange("p (h d) -> p h d", h=H),
                                             ALU.mult, ALU.add).then_inc(s.values_out, 1)

            def maxima(b, g):
                dve.wait_ge(s.top_scores, b.n * GP + g + 1)
                t, q = g // 4, g % 4
                dve.tensor_reduce(bm[:, t, MROW + 4 * q:MROW + 4 * q + 4],
                                  b_top[:, 0:4 * S2].rearrange("p (h k) -> p h k", h=4),
                                  AX, ALU.max).then_inc(s.maxima, 1)

            def normalise(b):
                dve.wait_ge(s.weighted_values, GP * (b.n + 1))
                if not (isinstance(b.n, int) and b.n < 1):
                    dve.wait_ge(s.attended_turned, b.n)
                ch = Chain(dve, s.attended_step, 1, b.n)
                o = [b_pv[t][:, 0:H * (DH + 1)].rearrange("p (h d) -> p h d", h=H) for t in range(QT)]
                dve.reciprocal(rden[:, 0], o[0][:, :, DH])
                ch.link(dve.reciprocal(rden[:, 1], o[1][:, :, DH]))
                for t in range(QT):
                    ins = dve.tensor_tensor(att[:, t].rearrange("p (h d) -> p h d", h=H), o[t][:, :, 0:DH],
                                            rden[:, t].unsqueeze(2).to_broadcast([P, H, DH]), ALU.mult)
                ins.then_inc(s.attended, 1)

            def residual(b):
                dve.wait_ge(s.attention_out, b.n + 1)
                dve.wait_ge(s.residual_base, b.n + 1)
                if b.layer == 0:
                    if not (isinstance(b.i, int) and b.i < 2):
                        dve.wait_ge(s_x1st[b.par], b.own * 16)
                elif not (isinstance(b.i, int) and b.i < 2):
                    dve.wait_ge(s.final_base, b.i - 1)
                gate = tgs[:, b.layer:b.layer + 1]
                dve.scalar_tensor_tensor(x1[:, b.par], b_proj[:].rearrange("p (t n) -> p t n", t=QT), gate,
                                         xb[:, b.par], ALU.mult, ALU.add).then_inc(s.row_update, 1)
                dve.wait_ge(s.row_update, b.n + 1)
                stats(1, x1, s.variance_after, b, b.par)

            def renorm(b):
                dve.wait_ge(s.root_after, b.n + 1)
                if b.layer == 0:
                    if not (isinstance(b.i, int) and b.i < 2):
                        dve.wait_ge(s_scat[b.par], b.own * 64)
                else:
                    if not (isinstance(b.n, int) and b.i < 2):
                        dve.wait_ge(s.normed_after_turned, b.n - 1)
                for t in range(QT):
                    ins = dve.tensor_scalar(h2[:, b.par, t], x1[:, b.par, t], mv[:, 1, t, 0:1],
                                            rstd[:, 1, t:t + 1], ALU.subtract, ALU.mult)
                ins.then_inc(s.normed_after, 1)

            def route(b):
                ch = Chain(dve, s.route_step, 5, b.i, wait_apart)
                dve.wait_ge(s.logits, b.i + 1)
                ch.link(dve.tensor_copy(lg[:], b_small[:, 0:QT * E].rearrange("p (t e) -> p t e", t=QT)))
                dve.max(top[:, 0], lg[:, 0])
                ch.link(dve.max(top[:, 1], lg[:, 1]))
                dve.max_index(topi[:, 0], top[:, 0], lg[:, 0])
                ch.link(dve.max_index(topi[:, 1], top[:, 1], lg[:, 1]))
                dve.tensor_tensor(gap[:, bass.ds(b.i, 1)].rearrange("p o t -> p (o t)"),
                                  top[:, :, 1], top[:, :, 0], ALU.subtract)
                ch.link(dve.tensor_copy(topf[:], topi[:]))
                for k in range(2):
                    ins = dve.tensor_tensor(oh[:, :, k],
                                            cst[:, C_IOTA:C_IOTA + E].unsqueeze(1).to_broadcast([P, QT, E]),
                                            topf[:, :, k:k + 1].to_broadcast([P, QT, E]), ALU.is_equal)
                ch.link(ins)
                dve.tensor_tensor(pick[:], oh[:, :, 0], oh[:, :, 1], ALU.add).then_inc(s.picked, 1)
                ch.end()

            def place(b):
                ch = Chain(dve, s.place_step, 4, b.i)
                dve.wait_ge(s.prefix, b.i + 1)
                ch.link(dve.tensor_tensor(rank[:], b_small[:, 16:32].rearrange("p (t e) -> p t e", t=QT),
                                          carry[:].unsqueeze(1).to_broadcast([P, QT, E]), ALU.add))
                dve.tensor_tensor(carry[:], carry[:], b_small[:, 32:40], ALU.add)
                for k in range(2):
                    ins = dve.tensor_tensor(sel2[:, :, k], oh[:, :, k], rank[:], ALU.mult)
                ch.link(ins)
                ch.link(dve.tensor_reduce(slotf[:], sel2[:], AX, ALU.add))
                if not (isinstance(b.i, int) and b.i < 2):
                    dve.wait_ge(s_scat[b.par], b.own * 64)
                ch.link(dve.tensor_copy(slot[:, b.par], slotf[:].rearrange("p t k -> p (t k)")))
                dve.tensor_copy(slots[:, bass.ds(b.i, 1)].rearrange("p o k -> p (o k)"),
                                slot[:, b.par]).then_inc(s.placed, 1)
                ch.end()

            def recall(b):
                if not (isinstance(b.i, int) and b.i < 2):
                    dve.wait_ge(s_gat[b.par], b.own * 64)
                dve.tensor_copy(slot[:, b.par],
                                slots[:, bass.ds(b.i, 1)].rearrange("p o k -> p (o k)")).then_inc(s.places_recalled, 1)

            def finish(b):
                dve.wait_ge(s.fourier_out, b.i + 1)
                dve.wait_ge(s.final_base, b.i + 1)
                if not (isinstance(b.i, int) and b.i < 2):
                    dve.wait_ge(s_ost[b.par], b.own * 16)
                dve.scalar_tensor_tensor(ob[:, b.par], b_proj[:].rearrange("p (t n) -> p t n", t=QT),
                                         tgs[:, 3:4], x3b[:, b.par], ALU.mult, ALU.add).then_inc(s.final_rows, 1)

            def front_low(b):
                low(hT[:, 1], hT[:, 0], b_t, s.normed_low, s.normed_high, b.n, 1.0)

            def q_low(b):
                low(qT[:, b.par, 1], qT[:, b.par, 0], b_proj, s.queries_low, s.queries_high, b.n, INV)

            def h2_low(b):
                low(h2s[:, 1], h2s[:, 0], b_t, s.normed_after_low, s.normed_after_high, b.n, 1.0)

            def step(b, front, tail, pre, ld):
                nx, pv = b.after(1), b.after(-1)
                if ld and b.layer == 1:
                    recall(b.after(3))
                if tail:
                    residual(pv)
                if front:
                    front_low(nx)
                if tail:
                    renorm(pv)
                if front:
                    q_low(nx)
                if pre:
                    pre_stats(b.after(2))
                if front:
                    maxima(nx, 0)
                if tail and b.layer == 1:
                    h2_low(pv)
                if front:
                    maxima(nx, 1)
                    maxima(nx, 2)
                if tail:
                    if b.layer == 0:
                        route(pv)
                    else:
                        finish(pv)
                if front:
                    for g in range(3, 6):
                        maxima(nx, g)
                if tail and b.layer == 0:
                    place(pv)
                if front:
                    maxima(nx, 6)
                normalise(b)
                if front:
                    maxima(nx, 7)
                if pre:
                    v_out(b.after(2))
                low(aT[:, 1], aT[:, 0], b_t, s.attended_low, s.attended_high, b.n, 1.0)
                if pre:
                    pre_norm(b.after(2))

            dve.wait_ge(s.consts_in, 16)
            dve.tensor_copy(identb[:], ident)
            dve.tensor_copy(utb[:], cst[:, C_UT:C_UT + P])
            dve.tensor_copy(oneb[:], cst[:, C_ONE:C_ONE + P])
            dve.tensor_copy(carry[:], cst[:, C_BASE:C_BASE + E])
            dve.tensor_copy(mhead[:], cst[0:MK, C_MH:C_END].rearrange("p (h k) -> p h k", h=H)).then_inc(s.consts_in, 1)
            dve.wait_ge(s.act_setup, 1)
            dve.tensor_scalar(tgs[:], tg[:], INV, None, ALU.mult)
            for k, g in ((0, 0), (1, 1), (2, 3)):
                dve.tensor_scalar(bias[:, k], bias[:, k], tg[:, g:g + 1], None, ALU.mult).then_inc(s.dve_setup, 1)
            for k in range(NW):
                dve.wait_ge(s.act_setup, k + 2)
                dve.scalar_tensor_tensor(wat[:, k, 1].rearrange("p c n -> p (c n)"), wst[:, k], SCALE,
                                         wat[:, k, 0].rearrange("p c n -> p (c n)"),
                                         ALU.mult, ALU.subtract).then_inc(s.dve_setup, 1)
            dve.wait_ge(s.act_setup, NW + 2)
            dve.tensor_tensor(ctxs[:, 1], ctx32, ctxs[:, 0], ALU.subtract).then_inc(s.dve_setup, 1)
            dve.wait_ge(s.act_setup, NW + 3)
            dve.scalar_tensor_tensor(bqz[0:1, 1], bqrow[0:1, :], SCALE, bqz[0:1, 0],
                                     ALU.mult, ALU.subtract).then_inc(s.dve_setup, 1)
            dve.wait_ge(s.fourier_read, 3)
            dve.scalar_tensor_tensor(mf[:, 1], b_f[2][:].rearrange("p (c n) -> p c n", c=KC), SCALE / D,
                                     mf[:, 0], ALU.mult, ALU.subtract).then_inc(s.dve_setup, 1)
            dve.wait_ge(s.pool_setup, 7)
            pre_stats(at(0, 0))
            pre_norm(at(0, 0), True)
            front_low(at(0, 0))
            pre_stats(at(0, 1))
            v_out(at(0, 0))
            q_low(at(0, 0))
            v_out(at(0, 1))
            for g in range(GP):
                maxima(at(0, 0), g)
            pre_norm(at(0, 1))
            steps(dve, 0, step)
            residual(at(0, 15))
            renorm(at(0, 15))
            route(at(0, 15))
            place(at(0, 15))

            ch = Chain(dve, s.count_step, 13 + 2 * E, 0)
            ch.link(dve.tensor_tensor(ntf[:], carry[:], cst[:, C_BASE:C_BASE + E], ALU.subtract))
            ch.link(dve.tensor_scalar(nti[:], ntf[:], float(S - 1), None, ALU.add))
            ch.link(dve.tensor_scalar(nti2[:], nti[:], 8, None, ALU.logical_shift_right))
            ch.link(dve.tensor_scalar(ntf[:], nti2[:], 1.0, None, ALU.max))
            ch.link(dve.memset(tsf[:], 0.0))
            ch.link(dve.memset(eqf[:, 0, 0:E], 1.0))
            ch.link(dve.tensor_tensor_scan(tsf[:, 1:E + 1], eqf[:, 0, 0:E], ntf[:], 0.0,
                                           ALU.mult, ALU.add))
            ch.link(dve.tensor_copy(tbl[0:1, 0:E + 1], tsf[0:1]))
            dve.tensor_copy(tbl[0:1, E + 1:2 * E + 1], carry[0:1, :]).then_inc(s.tiles_counted, 1)
            ch.link(dve.tensor_scalar(shift[:], ntf[:], float(S), -float(CAP), ALU.mult, ALU.add))
            ch.link(dve.tensor_copy(slotx[:], slots[:].rearrange("p b k -> p (b k)")))
            for e in range(1, E):
                src = slotx if e == 1 else slotz
                ch.link(dve.tensor_scalar(slott[:], slotx[:], float(e * CAP), shift[:, e - 1:e],
                                          ALU.is_ge, ALU.mult))
                ch.link(dve.tensor_tensor(slotz[:], src[:], slott[:], ALU.add))
            ch.link(dve.tensor_copy(slots[:].rearrange("p b k -> p (b k)"), slotz[:]))
            ch.link(dve.memset(wone[:], 0.0))
            dve.tensor_copy(wone[:, 0, 0:1], gap[:, 0, 0:1]).then_inc(s.gap_exponential, 1)
            dve.wait_ge(s.gap_exponential, 2)
            ch.link(dve.tensor_scalar(wone[:], wexp[:], 1.0, None, ALU.add))
            ch.link(dve.reciprocal(wone[:], wone[:]))
            ch.link(dve.tensor_scalar(wtok[:, :, :, 0], wone[:], tg[:, 2:3], None, ALU.mult))
            dve.tensor_tensor(wtok[:, :, :, 1], wtok[:, :, :, 0], wexp[:], ALU.mult).then_inc(s.token_weights, 1)

            dve.memset(ge, 0.0).then_inc(s.product, FC)
            dve.memset(a32, 0.0).then_inc(s.down, FC)
            dve.memset(xs, 0.0).then_inc(s.tile_turned, 1)
            dve.memset(ysb, 0.0).then_inc(s.expert_rows_stored, 16)
            dve.memset(xT, 0.0).then_inc(s.expert_rows, 2)
            dve.memset(act16, 0.0).then_inc(s.credits_given, 1)

            def x_low(g):
                dve.wait_ge(s.tile_high, g + 1)
                dve.tensor_tensor(xT[:, 1], b_t[:].rearrange("p (c n) -> p c n", c=KC), xT[:, 0],
                                  ALU.subtract).then_inc(s.tile_low, 1)

            dve.wait_ge(s.tiles_counted, 1)
            x_low(0)
            with dve.Fori(0, E) as e:
                t0 = dve.value_load(tbl[0:1, bass.ds(e, 1)], min_val=0, max_val=TILES)
                t1 = dve.value_load(tbl[0:1, bass.ds(e + 1, 1)], min_val=1, max_val=TILES)
                with dve.Fori(t0, t1) as g:
                    for fc in range(FC):
                        dve.wait_ge(s.gelu, g * FC + (fc + 1))
                        dve.scalar_tensor_tensor(a32[:, fc % 2], bank[1 + fc % 3][:, S:2 * S], INV,
                                                 ge[:, fc % 2], ALU.mult, ALU.mult).then_inc(s.product, 1)
                        dve.wait_ge(s.product, g * FC + (fc + 9))
                        dve.wait_ge(s.down, g * FC + (fc + 5))
                        dve.tensor_copy(act16[:, fc % 4, 0], a32[:, fc % 2]).then_inc(s.activation, 1)
                        dve.wait_ge(s.activation, g * (2 * FC) + (2 * fc + 1))
                        dve.tensor_tensor(act16[:, fc % 4, 1], a32[:, fc % 2], act16[:, fc % 4, 0],
                                          ALU.subtract).then_inc(s.activation, 1)
                    x_low(g + 1)

            for i in range(3):
                recall(at(1, i))
                if i == 0:
                    dve.wait_ge(s.token_weights, 1)
                if i == 1:
                    pre_stats(at(1, 0))
                    mask_rows(at(1, 0))
                    dve.tensor_copy(nfb[:], nf[:]).then_inc(s.unmasked_ready, 1)
                    pre_norm(at(1, 0))
            front_low(at(1, 0))
            v_out(at(1, 0))
            q_low(at(1, 0))
            v_out(at(1, 1))
            pre_stats(at(1, 1))
            for g in range(GP):
                maxima(at(1, 0), g)
            pre_norm(at(1, 1))
            steps(dve, 1, step)
            residual(at(1, 15))
            renorm(at(1, 15))
            h2_low(at(1, 15))
            finish(at(1, 15))

        @block.tensor
        def _(pe):
            def turn(dst, src):
                for c in range(KC):
                    for t in range(QT):
                        last = pe.transpose(dst[:, c * S + t * P:c * S + (t + 1) * P],
                                            src[:, t, c * P:(c + 1) * P], ident)
                return last

            def t_h(b):
                pe.wait_ge(s.normed, b.n + 1)
                turn(b_t, h).then_inc(s.normed_turned, 1)

            def t_h2(b):
                pe.wait_ge(s.normed_after, b.n + 1)
                turn(b_t, h2[:, b.par]).then_inc(s.normed_after_turned, 1)

            def proj_q(b):
                pe.wait_ge(s.normed_low, b.n + 1)
                for m in range(KC):
                    n = 0
                    total = 6 + (2 if b.layer else 0)
                    if b.layer:
                        for k in range(2):
                            pe.matmul(b_proj[:, m * S:(m + 1) * S], bqz[:, k, m * P:(m + 1) * P], nfT[:],
                                      start=n == 0, stop=False)
                            n += 1
                    for c in range(KC):
                        for i, j in PASSES:
                            n += 1
                            last = pe.matmul(b_proj[:, m * S:(m + 1) * S],
                                             wat[:, 4 * b.layer, i, c, m * P:(m + 1) * P], hT[:, j, c],
                                             start=n == 1, stop=n == total)
                last.then_inc(s.queries, 1)

            def proj_kv(b):
                for m in range(KC):
                    for n, (c, i, j) in enumerate([(c, i, j) for c in range(KC) for i, j in PASSES]):
                        pe.matmul(b_small[:, m * S2:(m + 1) * S2],
                                  wat[:, 4 * b.layer + 1, i, c, m * P:(m + 1) * P],
                                  ctxs[:, j, c, bass.ds(b.i * S2, S2)], start=n == 0, stop=n == 5)
                for n, (c, i, j) in enumerate([(c, i, j) for c in range(KC) for i, j in PASSES]):
                    last = pe.matmul(b_small[0:S2, 160:416], ctxs[:, i, c, bass.ds(b.i * S2, S2)],
                                     wat[:, 4 * b.layer + 2, j, c], start=n == 0, stop=n == 5)
                last.then_inc(s.keys_values, 1)

            def top_scores(b, g):
                t, q = g // 4, g % 4
                dst = b_top[:, 0:4 * S2]
                if g == 0:
                    pe.wait_ge(s.queries_high, b.n + 1)
                    pe.wait_ge(s.keys_diagonal, 2 * b.n + 2)
                    if not (isinstance(b.n, int) and b.n < 1):
                        pe.wait_ge(s.mask_ready, b.n)
                else:
                    pe.wait_ge(s.maxima, b.n * GP + g)
                pe.matmul(dst, qT[:, b.par, 0, q // 2, t * P:(t + 1) * P],
                          kbd[:, b.par, 0, q // 2, 4 * (q % 2):4 * (q % 2) + 4], start=True, stop=False)
                pe.matmul(dst, identb[:], bm[:, t, 0:S2].unsqueeze(1).to_broadcast([P, 4, S2]),
                          start=False, stop=True).then_inc(s.top_scores, 1)

            def t_mask(b):
                pe.wait_ge(s.maxima, GP * (b.n + 1))
                for t in range(QT):
                    last = pe.transpose(b_top[0:MK, 384 + 64 * t:384 + 64 * (t + 1)].bitcast(BF16),
                                        bm[:, t], identb[:])
                last.then_inc(s.mask_turned, 1)

            def scores(b, g):
                if g == 0:
                    pe.wait_ge(s.mask_ready, b.n + 1)
                    pe.wait_ge(s.queries_low, b.n + 1)
                if g >= 2:
                    pe.wait_ge(s.weights, b.n * GP + (g - 1))
                for j in range(2):
                    head = 2 * g + j
                    c, hh = head // HC, head % HC
                    dst = b_s[g % 2][0:S2, j * S:(j + 1) * S]
                    for n, (ki, qi) in enumerate(PASSES):
                        pe.matmul(dst, kbd[:, b.par, ki, c, hh], qT[:, b.par, qi, c], start=n == 0, stop=False)
                    last = pe.matmul(dst, mhead[:, head], mrhs[:], start=False, stop=True)
                last.then_inc(s.scores, 1)

            def values(b, g):
                if g == 0:
                    pe.wait_ge(s.values_out, b.n + 1)
                    if not (isinstance(b.n, int) and b.n < 1):
                        pe.wait_ge(s.attended, b.n)
                pe.wait_ge(s.weights, b.n * GP + (g + 1))
                for j in range(2):
                    head = 2 * g + j
                    for t in range(QT):
                        last = pe.matmul(b_pv[t][:, head * (DH + 1):(head + 1) * (DH + 1)],
                                         pr[0:S2, g % 4, j * S + t * P:j * S + (t + 1) * P],
                                         vaug[0:S2, b.par, head], start=True, stop=True)
                last.then_inc(s.weighted_values, 1)

            def t_att(b):
                pe.wait_ge(s.attended, b.n + 1)
                turn(b_t, att).then_inc(s.attended_turned, 1)

            def token_major(lhs, weight, done):
                for t in range(QT):
                    for n, (c, i, j) in enumerate([(c, i, j) for c in range(KC) for i, j in PASSES]):
                        last = pe.matmul(b_proj[:, t * D:(t + 1) * D], lhs[:, i, c, t * P:(t + 1) * P],
                                         weight[:, j, c], start=n == 0, stop=n == 5)
                last.then_inc(done, 1)

            def proj_o(b):
                pe.wait_ge(s.attended_low, b.n + 1)
                token_major(aT, wat[:, 4 * b.layer + 3], s.attention_out)

            def logits(b):
                for t in range(QT):
                    for c in range(KC):
                        last = pe.matmul(b_small[:, t * E:(t + 1) * E], h2T[:, c, t * P:(t + 1) * P],
                                         wg[:, c], start=c == 0, stop=c == KC - 1)
                last.then_inc(s.logits, 1)

            def prefix(b):
                pe.wait_ge(s.picked, b.i + 1)
                pe.matmul(b_small[:, 16:24], utb[:], pick[:, 0], start=True, stop=True)
                pe.matmul(b_small[:, 24:32], utb[:], pick[:, 1], start=True, stop=False)
                pe.matmul(b_small[:, 24:32], oneb[:], pick[:, 0], start=False, stop=True)
                pe.matmul(b_small[:, 32:40], oneb[:], pick[:, 0], start=True, stop=False)
                pe.matmul(b_small[:, 32:40], oneb[:], pick[:, 1], start=False, stop=True).then_inc(s.prefix, 1)

            def step(b, front, tail, pre, ld):
                nx, pv = b.after(1), b.after(-1)
                scores(b, 0)
                scores(b, 1)
                if tail:
                    if b.layer == 1 and not (isinstance(pv.i, int) and pv.i < 1):
                        pe.wait_ge(s.final_rows, pv.i)
                    proj_o(pv)
                values(b, 0)
                scores(b, 2)
                if front:
                    t_h(nx)
                values(b, 1)
                scores(b, 3)
                if front:
                    if tail:
                        pe.wait_ge(s.row_update, pv.n + 1)
                    proj_q(nx)
                values(b, 2)
                scores(b, 4)
                if tail:
                    if front:
                        pe.wait_ge(s.normed_low, nx.n + 1)
                    t_h2(pv)
                if front:
                    top_scores(nx, 0)
                values(b, 3)
                if front:
                    top_scores(nx, 1)
                scores(b, 5)
                if front:
                    top_scores(nx, 2)
                values(b, 4)
                if tail:
                    pe.wait_ge(s.normed_after_high, pv.n + 1)
                    if b.layer == 0:
                        if front:
                            pe.wait_ge(s.values_out, nx.n + 1)
                        logits(pv)
                    else:
                        pe.wait_ge(s.normed_after_low, pv.i + 1)
                        if front:
                            pe.wait_ge(s.queries_low, nx.n + 1)
                        token_major(h2s, mf, s.fourier_out)
                if front:
                    top_scores(nx, 3)
                scores(b, 6)
                values(b, 5)
                if front:
                    top_scores(nx, 4)
                scores(b, 7)
                if front:
                    top_scores(nx, 5)
                if tail and b.layer == 0:
                    prefix(pv)
                values(b, 6)
                if front:
                    top_scores(nx, 6)
                values(b, 7)
                if front:
                    top_scores(nx, 7)
                if pre:
                    if tail and b.layer == 0:
                        pe.wait_ge(s.placed, pv.i + 1)
                    else:
                        pe.wait_ge(s.values_out, nx.n + 1)
                    proj_kv(b.after(2))
                if front:
                    t_mask(nx)
                if tail:
                    pe.wait_ge(s.normed_after_high if b.layer == 0 else s.normed_after_low,
                               pv.n + 1 if b.layer == 0 else pv.i + 1)
                else:
                    pe.wait_ge(s.normed_low, nx.n + 1)
                t_att(b)

            pe.wait_ge(s.fourier_in, 16 * 5)
            for k, terms in enumerate((((0, 0), (1, 1)), ((1, 0), (0, 2)))):
                for m in range(KC):
                    for n, (c, w, f) in enumerate([(c, w, f) for c in range(KC) for w, f in terms]):
                        last = pe.matmul(b_f[k][:, m * D:(m + 1) * D], wf[:, w, c, m * P:(m + 1) * P],
                                         dft[:, f, c], start=n == 0, stop=n == 3)
                last.then_inc(s.fourier_product, 1)
            pe.wait_ge(s.fourier_read, 2)
            for m in range(KC):
                for n, (c, w) in enumerate([(c, w) for c in range(KC) for w in range(2)]):
                    last = pe.matmul(b_f[2][:, m * D:(m + 1) * D], afT[:, w, c, m * P:(m + 1) * P],
                                     dft[:, (0, 2)[w], c], start=n == 0, stop=n == 3)
            last.then_inc(s.fourier_product, 1)

            pe.wait_ge(s.consts_in, 17)
            pe.wait_ge(s.dve_setup, 3 + NW + 3)
            b0 = at(0, 0)
            t_h(b0)
            proj_kv(b0)
            proj_q(b0)
            pe.wait_ge(s.values_out, 1)
            proj_kv(at(0, 1))
            for g in range(GP):
                top_scores(b0, g)
            t_mask(b0)
            steps(pe, 0, step)
            last0 = at(0, 15)
            proj_o(last0)
            t_h2(last0)
            pe.wait_ge(s.normed_after_high, NB)
            logits(last0)
            prefix(last0)

            pe.wait_ge(s.tiles_counted, 1)
            pe.wait_ge(s.credits_given, 1)

            def t_x(g):
                pe.wait_ge(s.tile_in, g * 16 + 16)
                turn(b_t, xs).then_inc(s.tile_turned, 1)

            gate_up = we

            def up(par, g, fc):
                pe.wait_ge(s.product, g * FC + ((fc + 6) if fc >= 3 else (7, 8, 6)[fc]))
                for half in range(2):
                    col = half * F + fc * P
                    for n, (c, i, j) in enumerate([(c, i, j) for c in range(KC) for i, j in PASSES]):
                        last = pe.matmul(bank[1 + fc % 3][:, half * S:(half + 1) * S],
                                         gate_up[:, par, c, i, col:col + P], xT[:, j, c],
                                         start=n == 0, stop=n == 5)
                last.then_inc(s.gate_up, 1)

            def down(par, g, fc):
                if fc == 0:
                    pe.wait_ge(s.expert_rows, g * 2 + 2)
                pe.wait_ge(s.activation, g * (2 * FC) + (2 * fc + 2))
                for t in range(QT):
                    for n, (i, j) in enumerate(PASSES):
                        last = pe.matmul(bank[4 + t][:, 0:D], act16[:, fc % 4, i, t * P:(t + 1) * P],
                                         we[:, par, 2, j, fc * D:(fc + 1) * D],
                                         start=fc == 0 and n == 0, stop=fc == FC - 1 and n == 2)
                last.then_inc(s.down, 1)

            t_x(0)
            with pe.Fori(0, E // 2) as pair:
                for par in range(2):
                    e = pair * 2 + par
                    t0 = pe.value_load(tbl[0:1, bass.ds(e, 1)], min_val=0, max_val=TILES)
                    t1 = pe.value_load(tbl[0:1, bass.ds(e + 1, 1)], min_val=1, max_val=TILES)
                    with pe.Fori(t0, t1) as g:
                        pe.wait_ge(s.expert_weights, e * 3 + 3)
                        pe.wait_ge(s.tile_low, g + 1)
                        up(par, g, 0)
                        up(par, g, 1)
                        for fc in range(2, FC):
                            up(par, g, fc)
                            down(par, g, fc - 2)
                        t_x(g + 1)
                        down(par, g, FC - 2)
                        down(par, g, FC - 1)

            b1 = at(1, 0)
            t_h(b1)
            pe.wait_ge(s.unmasked_ready, 1)
            for t in range(QT):
                last = pe.transpose(b_top[0:1, 384 + 64 * t:384 + 64 * (t + 1)].bitcast(BF16),
                                    nfb[:, t:t + 1], identb[:])
            last.then_inc(s.unmasked_turned, 1)
            pe.wait_ge(s.unmasked_ready, 2)
            proj_kv(b1)
            proj_q(b1)
            pe.wait_ge(s.values_out, NB + 1)
            proj_kv(at(1, 1))
            for g in range(GP):
                top_scores(b1, g)
            t_mask(b1)
            steps(pe, 1, step)
            last1 = at(1, 15)
            pe.wait_ge(s.final_rows, NB - 1)
            proj_o(last1)
            t_h2(last1)
            pe.wait_ge(s.normed_after_low, NB)
            token_major(h2s, mf, s.fourier_out)


def tables():
    c = np.zeros((P, C_END), np.float32)
    r = np.arange(P)
    c[:, C_ID:C_ID + P] = np.eye(P)
    c[:, C_UT:C_UT + P] = r[:, None] < r[None, :]
    c[:, C_ONE:C_ONE + P] = 1.0
    c[:, C_SEL:C_SEL + HC] = r[:, None] // DH == np.arange(HC)[None, :]
    c[:, C_IOTA:C_IOTA + E] = np.arange(E)
    c[:, C_BASE:C_BASE + E] = np.arange(E) * CAP
    m = np.zeros((P, H, S2), np.float32)
    for k in range(S2):
        m[k, :, k] = 1.0
    for head in range(H):
        m[MROW + head, head, :] = -1.0
    c[:, C_MH:C_END] = m.reshape(P, -1)
    angle = 2.0 * np.pi * (np.outer(np.arange(D), np.arange(D)) % D) / D
    return c, np.cos(angle).astype(np.float32), np.sin(angle).astype(np.float32)


def kernel(**inputs):
    import concourse.bacc as bacc
    from concourse.bass_utils import run_bass_kernel_spmd as run

    arr = {k: np.asarray(v) for k, v in inputs.items()}
    consts, dcos, dsin = tables()
    laid = {
        "x": arr["x"], "mask0": arr["mask_Bx1xSxS2_if1"], "mask1": arr["mask_1x1xSxS2_ik0"],
        "consts": consts, "dcos": dcos, "dsin": dsin, "dnsin": tables()[2] * np.float32(-1),
        "ctxT": arr["ctx_1024"].transpose(2, 0, 1).reshape(D, NB * S2),
        "w0": arr["L0_xattn_Wq"].T, "w1": arr["L0_xattn_Wk"].T,
        "w2": arr["L0_xattn_Wv"].T, "w3": arr["L0_xattn_Wo"].T,
        "w4": arr["L1_xattn_wq_w"].T, "w5": arr["L1_xattn_wk_w"].T,
        "w6": arr["L1_xattn_wv_w"].T, "w7": arr["L1_xattn_wo_w"].T,
        "gates": np.concatenate([arr["g_xattn"], arr["g_ffn"]]),
        "bo0": arr["L0_xattn_bo"], "bo1": arr["L1_xattn_wo_b"], "fb": arr["L1_ffn_bias"],
        "bv": arr["L1_xattn_wv_b"], "bk": arr["L1_xattn_wk_b"].reshape(KC, P).T, "bq": arr["L1_xattn_wq_b"],
        "gwT": arr["L0_ffn_gate_w"].T,
        "guT": arr["L0_ffn_gate_up_w"].transpose(0, 2, 1).reshape(E * D, 2 * F),
        "dnT": arr["L0_ffn_down_w"].transpose(0, 2, 1).reshape(E * F, D),
        "wfr": arr["L1_ffn_w_freq_real"], "wfi": arr["L1_ffn_w_freq_imag"],
    }
    nc = bacc.Bacc("TRN2", target_bir_lowering=False, num_devices=1)
    arrays, args = {}, {}
    for name, value in laid.items():
        value = np.ascontiguousarray(value)
        arrays[f"in_{name}"] = value
        args[name] = nc.dram_tensor(f"in_{name}", value.shape, mybir.dt.from_np(value.dtype),
                                    kind="ExternalInput").ap()
    out = nc.dram_tensor("out_0", (NB, S, D), F32, kind="ExternalOutput").ap()
    build(nc, args, out)
    r = run(nc, [arrays], core_ids=[0])
    return r.results[0]["out_0"]
```

```python
from contextlib import ExitStack

import numpy as np

import concourse.bass as bass
from concourse import mybir

F32 = mybir.dt.float32
F16 = mybir.dt.float16
BF16 = mybir.dt.bfloat16
I32 = mybir.dt.int32
U32 = mybir.dt.uint32
ALU = mybir.AluOpType
ACT = mybir.ActivationFunctionType
AX = mybir.AxisListType.X

P = 128
NB, S, D = 16, 256, 256
S2 = 77
H, DH = 16, 16
KC = D // P
QT = S // P
HC = H // KC
E, F = 8, 1024
FC = F // P
TILES = 2 * NB + E
CAP = NB * S + S
SCALE = 64.0
INV = 1.0 / SCALE
BIG = 2.0 ** 100
EPS = 1e-5
ROOT = 0.25
MROW = 96
MK = MROW + H
GP = 2 * H // 4
NW = 8
PASSES = ((0, 0), (0, 1), (1, 0))
POOL_LOW = (5, 6)

C_ID, C_UT, C_ONE, C_SEL, C_IOTA, C_BASE, C_MH = 0, 128, 256, 384, 392, 400, 408
C_END = C_MH + H * S2


class Batch:

    def __init__(self, layer, i, half, par):
        self.i, self.par = i, par
        self.n = i + NB * layer
        self.half = half + NB // 2 * layer
        self.own = half
        self.layer, self._half = layer, half

    def after(self, k):
        up = (self.par + k) // 2
        return Batch(self.layer, self.i + k, self._half + up, (self.par + k) % 2)


def at(layer, i):
    return Batch(layer, i, i // 2, i % 2)


def steps(eng, layer, step):
    step(at(layer, 0), True, False, True, True)
    step(at(layer, 1), True, True, True, True)
    step(at(layer, 2), True, True, True, True)
    with eng.Fori(0, 5) as j:
        step(Batch(layer, j * 2 + 3, j + 1, 1), True, True, True, True)
        step(Batch(layer, j * 2 + 4, j + 2, 0), True, True, True, True)
    step(at(layer, 13), True, True, True, False)
    step(at(layer, 14), True, True, False, False)
    step(at(layer, 15), False, True, False, False)


class Signals:
    pass


class Chain:

    def __init__(self, eng, sem, per, i, wait=None):
        self.eng, self.sem, self.per, self.i, self.k = eng, sem, per, i, 0
        self.wait = wait or type(eng).wait_ge

    def link(self, ins):
        self.k += 1
        assert self.k <= self.per, self.sem
        ins.then_inc(self.sem, 1)
        self.wait(self.eng, self.sem, self.i * self.per + self.k)

    def end(self):
        assert self.k == self.per, (self.k, self.per)


def build(nc, a, out):
    x_d = a["x"].rearrange("b s d -> (b s) d")
    out_d = out.rearrange("b s d -> (b s) d")
    m0_d = a["mask0"].rearrange("b o s k -> (b o s) k")
    m1_d = a["mask1"].rearrange("b o s k -> (b o s) k")
    x1_d = nc.dram_tensor("x1_scratch", (NB * S, D), F32, kind="Internal").ap()
    xs_d = nc.dram_tensor("expert_in", (E * CAP, D), F32, kind="Internal").ap()
    ys_d = nc.dram_tensor("expert_out", (TILES * S, D), F32, kind="Internal").ap()

    def rows(dram, start):
        return dram[bass.ds(start, S), :].rearrange("(p t) d -> p t d", t=QT)

    def tile_row(e, g, t0):
        return nc.s_assert_within(e * CAP + g * S - t0 * S, 0, E * CAP - S,
                                  skip_runtime_bounds_check_because="an expert has at most NB * S rows")

    with ExitStack() as ctx:
        def sb(name, shape, dt):
            return ctx.enter_context(nc.sbuf_tensor(name, shape, dt))

        def sem(name):
            return ctx.enter_context(nc.semaphore(name))

        bank = [ctx.enter_context(nc.psum_tensor(f"bank{i}", [P, 512], F32)) for i in range(8)]
        b_t, b_proj, b_small = bank[0], bank[1], bank[2]
        b_s, b_top, b_pv = bank[3:5], bank[5], bank[6:8]
        b_f = bank[3:6]

        cst = sb("cst", [P, C_END], F32)
        ident = cst[:, C_ID:C_ID + P]
        identb = sb("identb", [P, P], BF16)
        utb = sb("utb", [P, P], BF16)
        oneb = sb("oneb", [P, P], BF16)
        mhead = sb("mhead", [MK, H, S2], BF16)
        mhalf = sb("mhalf", [P, QT], F32)
        cell = sb("cell", [1, 130], F32)
        gates = sb("gates", [P, 4], F32)
        tg = sb("tg", [P, 4], F32)
        tgs = sb("tgs", [P, 4], F32)
        we_flat = sb("we", [P, 2, 3 * 2 * 2048], F16)
        we = we_flat[:].rearrange("p b (k i n) -> p b k i n", k=3, i=2)
        early = we_flat[:, 1].bitcast(F32)
        wst = early[:, 0:NW * KC * D].rearrange("p (k n) -> p k n", k=NW)
        wat = sb("wat", [P, NW, 2, KC, D], F16)
        ctxs = sb("ctxs", [P, 2, KC, NB * S2], F16)
        bias = sb("bias", [P, 4, D], F32)
        bkq = sb("bkq", [P, KC], F32)
        bqrow = sb("bqrow", [P, D], F32)
        bqz = sb("bqz", [P, 2, D], F16)
        nfT = sb("nfT", [P, S], BF16)
        dft = sb("dft", [P, 3, KC, D], F32)
        mf = sb("mf", [P, 2, KC, D], F16)
        xin = sb("xin", [P, 2, QT, D], F32)
        mraw = sb("mraw", [P, 2, QT, S2], I32)
        xb = sb("xb", [P, 2, QT, D], F32)
        eqf = sb("eqf", [P, QT, S2], F32)
        full = sb("full", [P, QT], F32)
        nf = sb("nf", [P, QT], F32)
        nfb = sb("nfb", [P, QT], BF16)
        nbig = sb("nbig", [P, QT], F32)
        bm = sb("bm", [P, QT, MK], BF16)
        st = sb("st", [P, 2, QT, 6], F32)
        mv = sb("mv", [P, 2, QT, 2], F32)
        ve = sb("ve", [P, 2, QT], F32)
        rstd = sb("rstd", [P, 2, QT], F32)
        rq = sb("rq", [P, QT], F32)
        nq = sb("nq", [P, QT], F32)
        nr = sb("nr", [P, QT], F32)
        h = sb("h", [P, QT, D], F32)
        hT = sb("hT", [P, 2, KC, S], F16)
        qT = sb("qT", [P, 2, 2, KC, S], F16)
        kf = sb("kf", [P, KC, S2], F32)
        kp = sb("kp", [P, 2, KC, S2], F16)
        kbd = sb("kbd", [P, 2, 2, KC, HC, S2], F16)
        v32 = sb("v32", [P, H, DH], F32)
        vaug = sb("vaug", [P, 2, 2, H, DH + 1], F16)
        mrhs = sb("mrhs", [MK, S], BF16)
        pr32 = sb("pr32", [P, 2, 2 * S], F32)
        pr = sb("pr", [P, 4, 2, 2 * S], F16)
        rden = sb("rden", [P, QT, H], F32)
        att = sb("att", [P, QT, D], F32)
        aT = sb("aT", [P, 2, KC, S], F16)
        x1 = sb("x1", [P, 2, QT, D], F32)
        x3b = sb("x3b", [P, 2, QT, D], F32)
        h2 = sb("h2", [P, 2, QT, D], F32)
        h2T = sb("h2T", [P, KC, S], F32)
        h2s = sb("h2s", [P, 2, KC, S], F16)
        ob = sb("ob", [P, 2, QT, D], F32)
        wg = sb("wg", [P, KC, E], F32)
        lg = sb("lg", [P, QT, E], F32)
        top = sb("top", [P, QT, 8], F32)
        topi = sb("topi", [P, QT, 8], U32)
        topf = sb("topf", [P, QT, 8], F32)
        oh = sb("oh", [P, QT, 2, E], F32)
        pick = sb("pick", [P, QT, E], BF16)
        carry = sb("carry", [P, E], F32)
        rank = sb("rank", [P, QT, E], F32)
        sel2 = sb("sel2", [P, QT, 2, E], F32)
        slotf = sb("slotf", [P, QT, 2], F32)
        slot = sb("slot", [P, 2, QT * 2], I32)
        slots = sb("slots", [P, NB, QT * 2], I32)
        gap = sb("gap", [P, NB, QT], F32)
        wexp = sb("wexp", [P, NB, QT], F32)
        wone = sb("wone", [P, NB, QT], F32)
        wtok = sb("wtok", [P, NB, QT, 2], F32)
        wcur = sb("wcur", [P, 2, QT * 2], F32)
        yg = sb("yg", [P, 2, QT, 2, D], F32)
        nti = sb("nti", [P, E], I32)
        nti2 = sb("nti2", [P, E], I32)
        ntf = sb("ntf", [P, E], F32)
        tsf = sb("tsf", [P, E + 1], F32)
        shift = sb("shift", [P, E], F32)
        slotx = sb("slotx", [P, NB * QT * 2], F32)
        slott = sb("slott", [P, NB * QT * 2], F32)
        slotz = sb("slotz", [P, NB * QT * 2], F32)
        tbl = sb("tbl", [1, 2 * E + 1], I32)
        zeros = sb("zeros", [P, QT, D], F32)
        wes = sb("wes", [P, 1, 2048], F32)
        tiles = sb("tiles", [P, 3584], F32)
        xs = tiles[:, 0:512].rearrange("p (t n) -> p t n", t=QT)
        ysb = tiles[:, 512:1024].rearrange("p (t n) -> p t n", t=QT)
        xT = tiles[:, 1024:1536].bitcast(F16).rearrange("p (i c n) -> p i c n", i=2, c=KC)
        ge = tiles[:, 1536:2048].rearrange("p (b n) -> p b n", b=2)
        a32 = tiles[:, 2048:2560].rearrange("p (b n) -> p b n", b=2)
        act16 = tiles[:, 2560:3584].bitcast(F16).rearrange("p (b i n) -> p b i n", b=4, i=2)
        wf = tiles[:, 2560:3584].rearrange("p (k c n) -> p k c n", k=2, c=KC)
        afT = pr32[:].rearrange("p b (c n) -> p b c n", c=KC)
        ctx32 = tiles[:, 0:KC * NB * S2].rearrange("p (c n) -> p c n", c=KC)

        s = Signals()
        s.consts_in = sem("consts_in")
        s.context_in = sem("context_in")
        s.attention_weights_in = sem("attention_weights_in")
        s.late_weights_in = sem("late_weights_in")
        s.fourier_in = sem("fourier_in")
        s.small_inputs_in = sem("small_inputs_in")
        s.pool_setup = sem("pool_setup")
        s.dve_setup = sem("dve_setup")
        s.act_setup = sem("act_setup")
        s.fourier_product = sem("fourier_product")
        s.fourier_read = sem("fourier_read")
        s.unmasked_turned = sem("unmasked_turned")
        s.unmasked_ready = sem("unmasked_ready")
        s.rows_in_even = sem("rows_in_even")
        s.rows_in_odd = sem("rows_in_odd")
        s.variance = sem("variance")
        s.root = sem("root")
        s.variance_after = sem("variance_after")
        s.root_after = sem("root_after")
        s.residual_base = sem("residual_base")
        s.query_scale = sem("query_scale")
        s.normed = sem("normed")
        s.normed_turned = sem("normed_turned")
        s.normed_high = sem("normed_high")
        s.normed_low = sem("normed_low")
        s.queries = sem("queries")
        s.queries_high = sem("queries_high")
        s.queries_low = sem("queries_low")
        s.keys_values = sem("keys_values")
        s.keys_out = sem("keys_out")
        s.values_out = sem("values_out")
        s.values_high = sem("values_high")
        s.values_low = sem("values_low")
        s.keys_split = sem("keys_split")
        s.keys_diagonal = sem("keys_diagonal")
        s.top_scores = sem("top_scores")
        s.maxima = sem("maxima")
        s.mask_turned = sem("mask_turned")
        s.mask_ready = sem("mask_ready")
        s.scores = sem("scores")
        s.weights = sem("weights")
        s.weights_low = sem("weights_low")
        s.weights_low_pool = sem("weights_low_pool")
        s.weighted_values = sem("weighted_values")
        s.attended = sem("attended")
        s.attended_turned = sem("attended_turned")
        s.attended_high = sem("attended_high")
        s.attended_low = sem("attended_low")
        s.attention_out = sem("attention_out")
        s.row_update = sem("row_update")
        s.update_stored_even = sem("update_stored_even")
        s.update_stored_odd = sem("update_stored_odd")
        s.after_shift = sem("after_shift")
        s.normed_after = sem("normed_after")
        s.normed_after_turned = sem("normed_after_turned")
        s.normed_after_high = sem("normed_after_high")
        s.normed_after_low = sem("normed_after_low")
        s.table_zeroed = sem("table_zeroed")
        s.logits = sem("logits")
        s.picked = sem("picked")
        s.prefix = sem("prefix")
        s.placed = sem("placed")
        s.scattered_even = sem("scattered_even")
        s.scattered_odd = sem("scattered_odd")
        s.fourier_out = sem("fourier_out")
        s.final_base = sem("final_base")
        s.final_rows = sem("final_rows")
        s.final_stored_even = sem("final_stored_even")
        s.final_stored_odd = sem("final_stored_odd")
        s.gathered_even = sem("gathered_even")
        s.gathered_odd = sem("gathered_odd")
        s.experts_added = sem("experts_added")
        s.route_step = sem("route_step")
        s.place_step = sem("place_step")
        s.token_weights = sem("token_weights")
        s.mask_step = sem("mask_step")
        s.norm_step = sem("norm_step")
        s.attended_step = sem("attended_step")
        s.stats_step = sem("stats_step")
        s.stats_after_step = sem("stats_after_step")
        s.root_step = sem("root_step")
        s.root_after_step = sem("root_after_step")
        s.combine_step = sem("combine_step")
        s.places_recalled = sem("places_recalled")
        s.padding_zeroed = sem("padding_zeroed")
        s.tiles_counted = sem("tiles_counted")
        s.gap_exponential = sem("gap_exponential")
        s.expert_weights_in = sem("expert_weights_in")
        s.expert_weights = sem("expert_weights")
        s.first_high = sem("first_high")
        s.split_step = sem("split_step")
        s.tile_turned = sem("tile_turned")
        s.tile_in = sem("tile_in")
        s.tile_high = sem("tile_high")
        s.tile_low = sem("tile_low")
        s.gate_up = sem("gate_up")
        s.gelu = sem("gelu")
        s.product = sem("product")
        s.activation = sem("activation")
        s.down = sem("down")
        s.expert_rows = sem("expert_rows")
        s.expert_rows_stored = sem("expert_rows_stored")
        s.credits_given = sem("credits_given")
        s.count_step = sem("count_step")

        used = []

        def wait_apart(eng, which, value):
            eng.wait_ge(which, value)
            if not isinstance(value, int):
                used.append(1)
                n = 2 + len(used) % 128
                if eng is nc.vector:
                    eng.memset(cell[0:1, n:n + 1], 0.0)
                else:
                    eng.tensor_tensor(cell[0:1, n:n + 1], cell[0:1, 1:2], cell[0:1, 1:2], ALU.add)

        s_scat = (s.scattered_even, s.scattered_odd)
        s_gat = (s.gathered_even, s.gathered_odd)
        s_xin = (s.rows_in_even, s.rows_in_odd)
        s_x1st = (s.update_stored_even, s.update_stored_odd)
        s_ost = (s.final_stored_even, s.final_stored_odd)

        def a_place(g):
            return b_top[:, 0:4 * S2] if g % 2 == 0 else b_small[:, 0:4 * S2]

        def pad(eng, first, end):
            with eng.Fori(first, end) as e:
                row = eng.value_load(tbl[0:1, bass.ds(e + (E + 1), 1)], min_val=0, max_val=E * CAP - S)
                eng.dma_start(rows(xs_d, row), zeros[:]).then_inc(s.padding_zeroed, 16)

        def low_done(b, g):
            mine = [k for k in range(GP) if (k in POOL_LOW) == (g in POOL_LOW)]
            return (s.weights_low_pool if g in POOL_LOW else s.weights_low,
                    b.n * len(mine) + (mine.index(g) + 1))

        def weights_low(eng, b, g):
            if eng is nc.gpsimd:
                wait_apart(eng, s.weights, b.n * GP + g + 1)
            else:
                eng.wait_ge(s.weights, b.n * GP + g + 1)
            eng.tensor_tensor(pr[0:S2, g % 4, 1], pr32[0:S2, g % 2], pr[0:S2, g % 4, 0],
                              ALU.subtract).then_inc(low_done(b, g)[0], 1)

        block = ctx.enter_context(nc.Block())

        @block.sync
        def _(sp):
            def load(b):
                src = (x_d, x1_d)[b.layer]
                sp.dma_start(xin[:, b.par], rows(src, b.i * S)).then_inc(s_xin[b.par], 16)
                msk = rows(m0_d, b.i * S) if b.layer == 0 else rows(m1_d, 0)
                sp.dma_start(mraw[:, b.par], msk).then_inc(s_xin[b.par], 16)

            def load_weights(k, done):
                sp.dma_start(wst[:, k].rearrange("p (c n) -> p c n", c=KC),
                             a[f"w{k}"].rearrange("(c p) n -> p c n", p=P)).then_inc(done, 16)

            load(at(0, 0))
            sp.dma_start(cst[:], a["consts"]).then_inc(s.consts_in, 16)
            sp.dma_start(ctx32, a["ctxT"].rearrange("(c p) n -> p c n", p=P)).then_inc(s.context_in, 16)
            for k in range(NW // 2):
                load_weights(k, s.attention_weights_in)
            sp.dma_start(gates[:], a["gates"].partition_broadcast(P)).then_inc(s.small_inputs_in, 16)
            for k, name in enumerate(("bo0", "bo1", "fb", "bv")):
                sp.dma_start(bias[:, k], a[name].partition_broadcast(P)).then_inc(s.small_inputs_in, 16)
            sp.dma_start(bkq[:], a["bk"]).then_inc(s.small_inputs_in, 16)
            sp.dma_start(bqrow[0:1, :],
                         a["bq"].rearrange("(o d) -> o d", o=1)).then_inc(s.small_inputs_in, 16)
            sp.dma_start(wg[:], a["gwT"].rearrange("(c p) e -> p c e", p=P)).then_inc(s.small_inputs_in, 16)
            load(at(0, 1))
            for k in range(NW // 2, NW):
                load_weights(k, s.late_weights_in)
            for k, name in enumerate(("dcos", "dsin", "dnsin")):
                sp.dma_start(dft[:, k], a[name].rearrange("(c p) n -> p c n", p=P)).then_inc(s.fourier_in, 16)
            for k, name in enumerate(("wfr", "wfi")):
                sp.dma_start(wf[:, k], a[name].rearrange("(c p) n -> p c n", p=P)).then_inc(s.fourier_in, 16)

            def free_and_load(b):
                sp.wait_ge(s.normed, b.n - 1)
                sp.wait_ge(s.residual_base, b.n - 1)
                load(b)

            def step0(b, front, tail, pre, ld):
                if ld:
                    free_and_load(b.after(3))
                if tail:
                    keep(b.after(-1))

            def keep(b):
                sp.wait_ge(s.row_update, b.n + 1)
                sp.dma_start(rows(x1_d, b.i * S), x1[:, b.par]).then_inc(s_x1st[b.par], 16)

            free_and_load(at(0, 2))
            sp.wait_ge(s.pool_setup, 8)
            for k in range(5):
                n = TILES * S // P // 5
                dst = ys_d.rearrange("(k p t) d -> k p t d", k=5, p=P)[k]
                sp.dma_start(dst, zeros[:, 0:1].to_broadcast([P, n, D])).then_inc(s.table_zeroed, 16)
            steps(sp, 0, step0)
            keep(at(0, 15))

            for k in range(2):
                sp.wait_ge(s_x1st[k], 16 * (NB // 2))
            sp.wait_ge(s.tiles_counted, 1)
            pad(sp, E // 2, E)
            for k in range(2):
                sp.wait_ge(s_scat[k], 64 * (NB // 2))
            sp.wait_ge(s.padding_zeroed, 16 * E)
            with sp.Fori(0, E) as e:
                t0 = sp.value_load(tbl[0:1, bass.ds(e, 1)], min_val=0, max_val=TILES)
                t1 = sp.value_load(tbl[0:1, bass.ds(e + 1, 1)], min_val=1, max_val=TILES)
                with sp.Fori(t0, t1) as g:
                    sp.wait_ge(s.tile_turned, g + 1)
                    row = tile_row(e, g, t0)
                    sp.dma_start(xs, rows(xs_d, row)).then_inc(s.tile_in, 16)
            tend = sp.value_load(tbl[0:1, E:E + 1], min_val=1, max_val=TILES)
            sp.wait_ge(s.tile_turned, tend + 1)
            sp.dma_start(xs, rows(xs_d, 0)).then_inc(s.tile_in, 16)

            def step1(b, front, tail, pre, ld):
                if ld:
                    free_and_load(b.after(3))
                if tail:
                    store(b.after(-1))

            def store(b):
                sp.wait_ge(s.final_rows, b.i + 1)
                sp.dma_start(rows(out_d, b.i * S), ob[:, b.par]).then_inc(s_ost[b.par], 16)

            for i in range(3):
                free_and_load(at(1, i))
            steps(sp, 1, step1)
            store(at(1, 15))
            for k in range(2):
                sp.wait_ge(s_ost[k], 16 * (NB // 2))

        @block.gpsimd
        def _(pool):
            def weights(chunk, part, par, waited=None):
                ch = Chain(pool, s.split_step, 2, chunk - 3, wait_apart)
                stage = wes[:, 0]
                ch.link(pool.tensor_scalar(stage, stage, SCALE, 1.0, ALU.mult, ALU.mult))
                ch.link(pool.tensor_copy(we[:, par, part, 0], stage))
                pool.tensor_tensor(we[:, par, part, 1], stage, we[:, par, part, 0],
                                   ALU.subtract).then_inc(s.expert_weights, 1)

            def fetch(expert, part):
                if part < 2:
                    src = a["guT"][bass.ds(expert * D + part * P, P), :]
                else:
                    src = a["dnT"][bass.ds(expert * F, F), :].rearrange("(c p) n -> p c n", p=P)
                dst = wes[:, 0] if part < 2 else wes[:, 0].rearrange("p (c n) -> p c n", c=FC)
                pool.dma_start(dst, src).then_inc(s.expert_weights_in, 16)

            def ln_root(kind, count, done, b):
                ch = Chain(pool, (s.root_step, s.root_after_step)[kind], 1, b.n)
                wait_apart(pool, done, b.n + 1)
                ch.link(pool.tensor_scalar(ve[:, kind], mv[:, kind, :, 1], EPS, 1.0, ALU.add, ALU.mult))
                pool.tensor_tensor(rstd[:, kind], ve[:, kind], mhalf[:], ALU.pow).then_inc(count, 1)

            def base(b):
                pool.wait_ge(s_xin[b.par], 32 * (b.half + 1))
                if b.layer == 1:
                    pool.wait_ge(s.experts_added, b.i + 1)
                if not (isinstance(b.n, int) and b.n < 2):
                    pool.wait_ge(s.row_update, b.n - 1)
                pool.tensor_tensor(xb[:, b.par], xin[:, b.par],
                                   bias[:, b.layer].unsqueeze(1).to_broadcast([P, QT, D]),
                                   ALU.add).then_inc(s.residual_base, 1)

            def w_low(b, g):
                if g in POOL_LOW:
                    weights_low(pool, b, g)

            def root(b):
                ln_root(0, s.root, s.variance, b)

            def kdiag(b, k):
                if k == 0:
                    wait_apart(pool, s.keys_out, b.n + 1)
                    if not (isinstance(b.n, int) and b.n < 1):
                        wait_apart(pool, s.keys_diagonal, 2 * b.n)
                    pool.tensor_copy(kp[:, 0], kf[:]).then_inc(s.keys_split, 1)
                else:
                    pool.wait_ge(s.keys_split, 2 * b.n + 1)
                    pool.tensor_tensor(kp[:, 1], kf[:], kp[:, 0], ALU.subtract).then_inc(s.keys_split, 1)
                pool.wait_ge(s.keys_split, 2 * b.n + (k + 1))
                if k == 0 and not (isinstance(b.n, int) and b.n < 2):
                    pool.wait_ge(s.scores, GP * (b.n - 1))
                for c in range(KC):
                    ins = pool.tensor_tensor(
                        kbd[:, b.par, k, c],
                        kp[:, k, c].unsqueeze(1).to_broadcast([P, HC, S2]),
                        cst[:, C_SEL:C_SEL + HC].unsqueeze(2).to_broadcast([P, HC, S2]), ALU.mult)
                ins.then_inc(s.keys_diagonal, 1)

            def scatter(b, t):
                if t == 0:
                    wait_apart(pool, s.placed, b.i + 1)
                for k in range(2):
                    pool.indirect_dma_start(
                        out=xs_d, out_offset=bass.IndirectOffsetOnAxis(
                            ap=slot[:, b.par, 2 * t + k:2 * t + k + 1], axis=0),
                        in_=h2[:, b.par, t], in_offset=None).then_inc(s_scat[b.par], 16)

            def gather(b):
                wait_apart(pool, s.places_recalled, b.i + 1)
                for t in range(QT):
                    for k in range(2):
                        pool.indirect_dma_start(
                            out=yg[:, b.par, t, k], out_offset=None, in_=ys_d,
                            in_offset=bass.IndirectOffsetOnAxis(
                                ap=slot[:, b.par, 2 * t + k:2 * t + k + 1],
                                axis=0)).then_inc(s_gat[b.par], 16)

            def residual3(b):
                pool.wait_ge(s.row_update, b.n + 1)
                if not (isinstance(b.i, int) and b.i < 2):
                    pool.wait_ge(s.final_rows, b.i - 1)
                pool.tensor_tensor(x3b[:, b.par], x1[:, b.par],
                                   bias[:, 2].unsqueeze(1).to_broadcast([P, QT, D]),
                                   ALU.add).then_inc(s.final_base, 1)

            def step(b, front, tail, pre, ld):
                pv = b.after(-1)
                if front:
                    kdiag(b.after(1), 0)
                if b.layer == 0 and isinstance(b.i, int) and b.i in (14, 15):
                    pool.wait_ge(s.expert_weights, b.i - 13)
                    fetch(0, b.i - 13)
                late = b.layer == 0 and not (isinstance(b.i, int) and b.i < 2)
                if late:
                    scatter(b.after(-2), 0)
                if ld and b.layer == 1:
                    gather(b.after(3))
                if tail:
                    ln_root(1, s.root_after, s.variance_after, pv)
                if tail and b.layer == 1:
                    residual3(pv)
                if front and b.layer == 1:
                    base(b.after(1))
                if late:
                    scatter(b.after(-2), 1)
                if pre:
                    root(b.after(2))
                w_low(b, 5)
                w_low(b, 6)
                if front:
                    kdiag(b.after(1), 1)
                if front and b.layer == 0:
                    base(b.after(1))

            pool.memset(cell[0:1, 1:2], 0.0).then_inc(s.pool_setup, 1)
            pool.memset(mhalf[:], -0.5).then_inc(s.pool_setup, 1)
            pool.memset(zeros[:], 0.0).then_inc(s.pool_setup, 1)
            pool.memset(bm[:], 0.0).then_inc(s.pool_setup, 1)
            pool.memset(nfT[:], 0.0).then_inc(s.pool_setup, 1)
            pool.memset(bqz[:], 0.0).then_inc(s.pool_setup, 1)
            pool.memset(vaug[:, :, 0], 1.0).then_inc(s.pool_setup, 1)
            pool.memset(vaug[:, :, 1], 0.0).then_inc(s.pool_setup, 1)
            pool.wait_ge(s.pool_setup, 8)
            pool.wait_ge(s.consts_in, 16)
            pool.wait_ge(s.dve_setup, 3)
            root(at(0, 0))
            kdiag(at(0, 0), 0)
            kdiag(at(0, 0), 1)
            base(at(0, 0))
            root(at(0, 1))
            fetch(0, 0)
            steps(pool, 0, step)
            ln_root(1, s.root_after, s.variance_after, at(0, 15))
            for i in (14, 15):
                for t in range(QT):
                    scatter(at(0, i), t)

            pool.wait_ge(s.tiles_counted, 1)
            def expert(e, par, first=False):
                for part in range(3):
                    chunk = e * 3 + part
                    pool.wait_ge(s.expert_weights, chunk)
                    if not first and part == 0:
                        gone = pool.value_load(tbl[0:1, bass.ds(e - 1, 1)], min_val=1, max_val=TILES)
                        pool.wait_ge(s.down, gone * FC + FC)
                    fetch(e, part)
                    wait_apart(pool, s.expert_weights_in, (chunk + 1) * 16)
                    weights(chunk, part, par)

            expert(1, 1, True)
            with pool.Fori(1, E // 2) as pair:
                expert(pair * 2, 0)
                expert(pair * 2 + 1, 1)

            tend = pool.value_load(tbl[0:1, E:E + 1], min_val=1, max_val=TILES)
            wait_apart(pool, s.expert_rows_stored, (tend + 1) * 16)
            gather(at(1, 0))
            kdiag(at(1, 0), 0)
            root(at(1, 0))
            gather(at(1, 1))
            kdiag(at(1, 0), 1)
            base(at(1, 0))
            gather(at(1, 2))
            root(at(1, 1))
            steps(pool, 1, step)
            ln_root(1, s.root_after, s.variance_after, at(1, 15))
            residual3(at(1, 15))

        @block.scalar
        def _(act):
            def h_hi(b):
                act.wait_ge(s.normed_turned, b.n + 1)
                act.activation(hT[:, 0], b_t[:].rearrange("p (c n) -> p c n", c=KC),
                               ACT.Copy).then_inc(s.normed_high, 1)

            def h_norm(b):
                act.wait_ge(s.query_scale, b.n + 1)
                if not (isinstance(b.n, int) and b.n < 1):
                    act.wait_ge(s.normed_turned, b.n)
                for t in range(QT):
                    ins = act.activation(h[:, t], xin[:, b.par, t], ACT.Identity,
                                         bias=nq[:, t:t + 1], scale=rq[:, t:t + 1])
                ins.then_inc(s.normed, 1)

            def h2_norm(b):
                act.wait_ge(s.after_shift, b.n + 1)
                if b.layer == 0:
                    if not (isinstance(b.i, int) and b.i < 2):
                        act.wait_ge(s_scat[b.par], b.own * 64)
                else:
                    if not (isinstance(b.i, int) and b.i < 2):
                        act.wait_ge(s.normed_after_turned, b.n - 1)
                for t in range(QT):
                    ins = act.activation(h2[:, b.par, t], x1[:, b.par, t], ACT.Identity,
                                         bias=nr[:, t:t + 1], scale=rstd[:, 1, t:t + 1])
                ins.then_inc(s.normed_after, 1)

            def q_hi(b):
                act.wait_ge(s.queries, b.n + 1)
                if not (isinstance(b.n, int) and b.n < 2):
                    act.wait_ge(s.scores, GP * (b.n - 1))
                act.activation(qT[:, b.par, 0], b_proj[:].rearrange("p (c n) -> p c n", c=KC),
                               ACT.Copy, scale=INV).then_inc(s.queries_high, 1)

            def k_out(b):
                act.wait_ge(s.keys_values, b.n + 1)
                if not (isinstance(b.n, int) and b.n < 1):
                    act.wait_ge(s.keys_split, 2 * b.n)
                for c in range(KC):
                    ins = act.activation(kf[:, c], b_small[:, c * S2:(c + 1) * S2], ACT.Identity,
                                         bias=bkq[:, c:c + 1] if b.layer else 0.0, scale=INV)
                ins.then_inc(s.keys_out, 1)

            def m_out(b):
                act.wait_ge(s.mask_turned, b.n + 1)
                act.activation(mrhs[:], b_top[0:MK, 384:512].bitcast(BF16),
                               ACT.Copy).then_inc(s.mask_ready, 1)

            def expo(b, g):
                act.wait_ge(s.scores, b.n * GP + g + 1)
                if not (isinstance(b.n, int) and b.n * GP + g < 2):
                    act.wait_ge(*(low_done(b, g - 2) if g >= 2 else low_done(b.after(-1), g - 2 + GP)))
                if not (isinstance(b.n, int) and b.n * GP + g < 4):
                    act.wait_ge(s.weighted_values, b.n * GP + (g - 3))
                act.activation(pr32[0:S2, g % 2], b_s[g % 2][0:S2, :], ACT.Exp, scale=ROOT)
                act.activation(pr[0:S2, g % 4, 0], b_s[g % 2][0:S2, :], ACT.Exp,
                               scale=ROOT).then_inc(s.weights, 1)

            def v_hi(b):
                act.wait_ge(s.values_out, b.n + 1)
                if not (isinstance(b.n, int) and b.n < 2):
                    act.wait_ge(s.weighted_values, GP * (b.n - 1))
                act.activation(vaug[0:S2, b.par, 0, :, 0:DH], v32[0:S2], ACT.Copy).then_inc(s.values_high, 1)

            def tail_out(b):
                act.wait_ge(s.normed_after_turned, b.n + 1)
                src = b_t[:].rearrange("p (c n) -> p c n", c=KC)
                dst = h2T[:] if b.layer == 0 else h2s[:, 0]
                act.activation(dst, src, ACT.Copy).then_inc(s.normed_after_high, 1)

            def a_hi(b):
                act.wait_ge(s.attended_turned, b.n + 1)
                act.activation(aT[:, 0], b_t[:].rearrange("p (c n) -> p c n", c=KC),
                               ACT.Copy).then_inc(s.attended_high, 1)

            def first_expert(part):
                act.wait_ge(s.expert_weights_in, 16 * (part + 1))
                act.activation(we[:, 0, part, 0], wes[:, 0], ACT.Copy, scale=SCALE).then_inc(s.first_high, 1)

            def step(b, front, tail, pre, ld):
                nx, pv = b.after(1), b.after(-1)
                expo(b, 0)
                if tail:
                    a_hi(pv)
                expo(b, 1)
                if front:
                    v_hi(nx)
                expo(b, 2)
                if front:
                    h_hi(nx)
                expo(b, 3)
                expo(b, 4)
                if front:
                    q_hi(nx)
                if tail:
                    h2_norm(pv)
                expo(b, 5)
                if tail:
                    tail_out(pv)
                expo(b, 6)
                expo(b, 7)
                if pre:
                    h_norm(b.after(2))
                if front:
                    m_out(nx)
                if pre:
                    k_out(b.after(2))
                if b.layer == 0 and isinstance(b.i, int) and b.i >= 13:
                    first_expert(b.i - 13)

            act.wait_ge(s.small_inputs_in, 16 * 8)
            act.activation(tg[:], gates[:], ACT.Tanh).then_inc(s.act_setup, 1)
            def weights_high(k):
                act.activation(wat[:, k, 0].rearrange("p c n -> p (c n)"), wst[:, k], ACT.Copy,
                               scale=SCALE).then_inc(s.act_setup, 1)

            act.wait_ge(s.attention_weights_in, 16 * NW // 2)
            for k in range(NW // 2):
                weights_high(k)
            act.wait_ge(s.context_in, 16)
            act.activation(ctxs[:, 0], ctx32, ACT.Copy).then_inc(s.act_setup, 1)
            act.wait_ge(s.pool_setup, 6)
            act.activation(bqz[0:1, 0], bqrow[0:1, :], ACT.Copy, scale=SCALE).then_inc(s.act_setup, 1)
            h_norm(at(0, 0))
            h_hi(at(0, 0))
            k_out(at(0, 0))
            v_hi(at(0, 0))
            q_hi(at(0, 0))
            k_out(at(0, 1))
            m_out(at(0, 0))
            h_norm(at(0, 1))
            act.wait_ge(s.late_weights_in, 16 * NW // 2)
            for k in range(NW // 2, NW):
                weights_high(k)
            steps(act, 0, step)
            a_hi(at(0, 15))
            h2_norm(at(0, 15))
            tail_out(at(0, 15))
            act.wait_ge(s.tiles_counted, 1)
            pad(act, 0, E // 2)
            for k in range(2):
                act.wait_ge(s.fourier_product, k + 1)
                act.activation(afT[:, k], b_f[k][:].rearrange("p (c n) -> p c n", c=KC),
                               ACT.Copy).then_inc(s.fourier_read, 1)
            act.wait_ge(s.fourier_product, 3)
            act.activation(mf[:, 0], b_f[2][:].rearrange("p (c n) -> p c n", c=KC), ACT.Copy,
                           scale=SCALE / D).then_inc(s.fourier_read, 1)
            act.wait_ge(s.gap_exponential, 1)
            act.activation(wexp[:], gap[:], ACT.Exp).then_inc(s.gap_exponential, 1)

            def x_hi(g):
                act.wait_ge(s.tile_turned, g + 2)
                act.activation(xT[:, 0], b_t[:].rearrange("p (c n) -> p c n", c=KC),
                               ACT.Copy).then_inc(s.tile_high, 1)

            act.wait_ge(s.credits_given, 1)
            act.wait_ge(s.table_zeroed, 16 * 5)
            x_hi(0)
            with act.Fori(0, E) as e:
                t0 = act.value_load(tbl[0:1, bass.ds(e, 1)], min_val=0, max_val=TILES)
                t1 = act.value_load(tbl[0:1, bass.ds(e + 1, 1)], min_val=1, max_val=TILES)
                with act.Fori(t0, t1) as g:
                    for fc in range(FC):
                        act.wait_ge(s.gate_up, g * FC + (fc + 1))
                        act.wait_ge(s.product, g * FC + (fc + 7))
                        act.activation(ge[:, fc % 2], bank[1 + fc % 3][:, 0:S], ACT.Gelu,
                                       scale=INV).then_inc(s.gelu, 1)
                    x_hi(g + 1)
                    act.wait_ge(s.down, g * FC + 2 * FC)
                    act.wait_ge(s.expert_rows_stored, g * 16 + 16)
                    for t in range(QT):
                        act.activation(ysb[:, t], bank[4 + t][:, 0:D], ACT.Copy,
                                       scale=INV).then_inc(s.expert_rows, 1)
                    act.wait_ge(s.expert_rows, g * 2 + 4)
                    act.dma_start(rows(ys_d, g * S), ysb).then_inc(s.expert_rows_stored, 16)

            k_out(at(1, 0))
            h_norm(at(1, 0))
            h_hi(at(1, 0))
            act.wait_ge(s.unmasked_turned, 1)
            act.activation(nfT[0:1, :], b_top[0:1, 384:512].bitcast(BF16),
                           ACT.Copy).then_inc(s.unmasked_ready, 1)
            v_hi(at(1, 0))
            q_hi(at(1, 0))
            k_out(at(1, 1))
            m_out(at(1, 0))
            h_norm(at(1, 1))
            steps(act, 1, step)
            a_hi(at(1, 15))
            h2_norm(at(1, 15))
            tail_out(at(1, 15))

        @block.vector
        def _(dve):
            def stats(kind, src, sem_done, b, par):
                ch = Chain(dve, (s.stats_step, s.stats_after_step)[kind], 1, b.n, wait_apart)
                dve.bn_stats(st[:, kind, 0], src[:, par, 0])
                ch.link(dve.bn_stats(st[:, kind, 1], src[:, par, 1]))
                dve.bn_aggr(mv[:, kind, 0], st[:, kind, 0])
                dve.bn_aggr(mv[:, kind, 1], st[:, kind, 1]).then_inc(sem_done, 1)

            def combine(b):
                dve.wait_ge(s_xin[b.par], 32 * (b.half + 1))
                dve.wait_ge(s_gat[b.par], b.own * 64 + 64)
                dve.tensor_copy(wcur[:, b.par], wtok[:, bass.ds(b.i, 1)].rearrange(
                    "p o t k -> p (o t k)")).then_inc(s.combine_step, 1)
                dve.wait_ge(s.combine_step, b.i * 3 + 1)
                for k in range(2):
                    for t in range(QT):
                        ins = dve.scalar_tensor_tensor(
                            xin[:, b.par, t], yg[:, b.par, t, k],
                            wcur[:, b.par, 2 * t + k:2 * t + k + 1], xin[:, b.par, t],
                            ALU.mult, ALU.add)
                    ins.then_inc(s.combine_step, 1)
                    dve.wait_ge(s.combine_step, b.i * 3 + k + 2)
                dve.tensor_copy(zeros[:, 0, 0:1], wcur[:, b.par, 0:1]).then_inc(s.experts_added, 1)

            def pre_stats(b):
                if b.layer == 0:
                    dve.wait_ge(s_xin[b.par], 32 * (b.half + 1))
                else:
                    dve.wait_ge(s.combine_step, b.i * 3 + 3)
                stats(0, xin, s.variance, b, b.par)

            def mask_flags(b):
                ch = Chain(dve, s.mask_step, 3, b.n)
                ch.link(dve.tensor_scalar(eqf[:], mraw[:, b.par], 0, None, ALU.is_equal))
                ch.link(dve.tensor_reduce(full[:], eqf[:], AX, ALU.min))
                dve.tensor_scalar(nbig[:], full[:], BIG, -BIG, ALU.mult, ALU.add)
                ch.link(dve.tensor_scalar(nf[:], full[:], -1.0, 1.0, ALU.mult, ALU.add))

            def mask_rows(b, first=False):
                if not first:
                    dve.wait_ge(s.mask_turned, b.n)
                dve.tensor_tensor(bm[:, :, 0:S2], eqf[:],
                                  nbig[:].unsqueeze(2).to_broadcast([P, QT, S2]), ALU.mult)

            def pre_norm(b, first=False):
                ch = Chain(dve, s.norm_step, 1, b.n)
                dve.wait_ge(s.root, b.n + 1)
                if not first:
                    dve.wait_ge(s.normed, b.n)
                ch.link(dve.tensor_tensor(rq[:], rstd[:, 0], nf[:], ALU.mult))
                dve.scalar_tensor_tensor(nq[:], mv[:, 0, :, 0], -1.0, rq[:],
                                         ALU.mult, ALU.mult).then_inc(s.query_scale, 1)

            def low(dst, hi, src, done, hi_done, n, scale):
                dve.wait_ge(hi_done, n + 1)
                dve.scalar_tensor_tensor(dst, src[:].rearrange("p (c n) -> p c n", c=KC), scale, hi,
                                         ALU.mult, ALU.subtract).then_inc(done, 1)

            def v_out(b):
                dve.wait_ge(s.keys_out, b.n + 1)
                if not (isinstance(b.n, int) and b.n < 1):
                    dve.wait_ge(s.values_low, b.n)
                dst = v32[0:S2]
                src = b_small[0:S2, 160:416].rearrange("p (h d) -> p h d", h=H)
                if b.layer == 0:
                    dve.tensor_scalar(dst, src, INV, None, ALU.mult).then_inc(s.values_out, 1)
                else:
                    dve.scalar_tensor_tensor(dst, src, INV,
                                             bias[0:S2, 3].rearrange("p (h d) -> p h d", h=H),
                                             ALU.mult, ALU.add).then_inc(s.values_out, 1)

            def v_low(b):
                dve.wait_ge(s.values_high, b.n + 1)
                dve.tensor_tensor(vaug[0:S2, b.par, 1, :, 0:DH], v32[0:S2], vaug[0:S2, b.par, 0, :, 0:DH],
                                  ALU.subtract).then_inc(s.values_low, 1)

            def w_low(b, g):
                if g not in POOL_LOW:
                    weights_low(dve, b, g)

            def maxima(b, g):
                dve.wait_ge(s.top_scores, b.n * GP + g + 1)
                t, q = g // 4, g % 4
                dve.tensor_reduce(bm[:, t, MROW + 4 * q:MROW + 4 * q + 4],
                                  a_place(g).rearrange("p (h k) -> p h k", h=4),
                                  AX, ALU.max).then_inc(s.maxima, 1)

            def normalise(b):
                dve.wait_ge(s.weighted_values, GP * (b.n + 1))
                if not (isinstance(b.n, int) and b.n < 1):
                    dve.wait_ge(s.attended_turned, b.n)
                ch = Chain(dve, s.attended_step, 1, b.n)
                o = [b_pv[t][:, 0:H * (DH + 1)].rearrange("p (h d) -> p h d", h=H) for t in range(QT)]
                dve.reciprocal(rden[:, 0], o[0][:, :, DH])
                ch.link(dve.reciprocal(rden[:, 1], o[1][:, :, DH]))
                for t in range(QT):
                    ins = dve.tensor_tensor(att[:, t].rearrange("p (h d) -> p h d", h=H), o[t][:, :, 0:DH],
                                            rden[:, t].unsqueeze(2).to_broadcast([P, H, DH]), ALU.mult)
                ins.then_inc(s.attended, 1)

            def residual(b):
                dve.wait_ge(s.attention_out, b.n + 1)
                dve.wait_ge(s.residual_base, b.n + 1)
                if b.layer == 0:
                    if not (isinstance(b.i, int) and b.i < 2):
                        dve.wait_ge(s_x1st[b.par], b.own * 16)
                elif not (isinstance(b.i, int) and b.i < 2):
                    dve.wait_ge(s.final_base, b.i - 1)
                gate = tgs[:, b.layer:b.layer + 1]
                dve.scalar_tensor_tensor(x1[:, b.par], b_proj[:].rearrange("p (t n) -> p t n", t=QT), gate,
                                         xb[:, b.par], ALU.mult, ALU.add).then_inc(s.row_update, 1)
                dve.wait_ge(s.row_update, b.n + 1)
                stats(1, x1, s.variance_after, b, b.par)

            def renorm(b):
                dve.wait_ge(s.root_after, b.n + 1)
                dve.scalar_tensor_tensor(nr[:], mv[:, 1, :, 0], -1.0, rstd[:, 1],
                                         ALU.mult, ALU.mult).then_inc(s.after_shift, 1)

            def route(b):
                ch = Chain(dve, s.route_step, 5, b.i, wait_apart)
                dve.wait_ge(s.logits, b.i + 1)
                ch.link(dve.tensor_copy(lg[:], b_proj[:, 0:QT * E].rearrange("p (t e) -> p t e", t=QT)))
                dve.max(top[:, 0], lg[:, 0])
                ch.link(dve.max(top[:, 1], lg[:, 1]))
                dve.max_index(topi[:, 0], top[:, 0], lg[:, 0])
                ch.link(dve.max_index(topi[:, 1], top[:, 1], lg[:, 1]))
                dve.tensor_tensor(gap[:, bass.ds(b.i, 1)].rearrange("p o t -> p (o t)"),
                                  top[:, :, 1], top[:, :, 0], ALU.subtract)
                ch.link(dve.tensor_copy(topf[:], topi[:]))
                for k in range(2):
                    ins = dve.tensor_tensor(oh[:, :, k],
                                            cst[:, C_IOTA:C_IOTA + E].unsqueeze(1).to_broadcast([P, QT, E]),
                                            topf[:, :, k:k + 1].to_broadcast([P, QT, E]), ALU.is_equal)
                ch.link(ins)
                dve.tensor_tensor(pick[:], oh[:, :, 0], oh[:, :, 1], ALU.add).then_inc(s.picked, 1)
                ch.end()

            def place(b):
                ch = Chain(dve, s.place_step, 4, b.i)
                dve.wait_ge(s.prefix, b.i + 1)
                ch.link(dve.tensor_tensor(rank[:], b_proj[:, 16:32].rearrange("p (t e) -> p t e", t=QT),
                                          carry[:].unsqueeze(1).to_broadcast([P, QT, E]), ALU.add))
                dve.tensor_tensor(carry[:], carry[:], b_proj[:, 32:40], ALU.add)
                for k in range(2):
                    ins = dve.tensor_tensor(sel2[:, :, k], oh[:, :, k], rank[:], ALU.mult)
                ch.link(ins)
                ch.link(dve.tensor_reduce(slotf[:], sel2[:], AX, ALU.add))
                if not (isinstance(b.i, int) and b.i < 2):
                    dve.wait_ge(s_scat[b.par], b.own * 64)
                ch.link(dve.tensor_copy(slot[:, b.par], slotf[:].rearrange("p t k -> p (t k)")))
                dve.tensor_copy(slots[:, bass.ds(b.i, 1)].rearrange("p o k -> p (o k)"),
                                slot[:, b.par]).then_inc(s.placed, 1)
                ch.end()

            def recall(b):
                if not (isinstance(b.i, int) and b.i < 2):
                    dve.wait_ge(s_gat[b.par], b.own * 64)
                place = slots[:, bass.ds(b.i, 1)].rearrange("p o k -> p (o k)")
                dve.tensor_copy(slot[:, b.par], place).then_inc(s.places_recalled, 1)

            def finish(b):
                dve.wait_ge(s.fourier_out, b.i + 1)
                dve.wait_ge(s.final_base, b.i + 1)
                if not (isinstance(b.i, int) and b.i < 2):
                    dve.wait_ge(s_ost[b.par], b.own * 16)
                dve.scalar_tensor_tensor(ob[:, b.par], b_proj[:].rearrange("p (t n) -> p t n", t=QT),
                                         tgs[:, 3:4], x3b[:, b.par],
                                         ALU.mult, ALU.add).then_inc(s.final_rows, 1)

            def front_low(b):
                low(hT[:, 1], hT[:, 0], b_t, s.normed_low, s.normed_high, b.n, 1.0)

            def q_low(b):
                low(qT[:, b.par, 1], qT[:, b.par, 0], b_proj, s.queries_low, s.queries_high, b.n, INV)

            def a_low(b):
                low(aT[:, 1], aT[:, 0], b_t, s.attended_low, s.attended_high, b.n, 1.0)

            def h2_low(b):
                low(h2s[:, 1], h2s[:, 0], b_t, s.normed_after_low, s.normed_after_high, b.n, 1.0)

            def step(b, front, tail, pre, ld):
                nx, pv = b.after(1), b.after(-1)
                if ld and b.layer == 1:
                    recall(b.after(3))
                w_low(b, 0)
                if tail:
                    a_low(pv)
                w_low(b, 1)
                if front:
                    v_low(nx)
                w_low(b, 2)
                if front:
                    front_low(nx)
                if tail:
                    residual(pv)
                w_low(b, 3)
                w_low(b, 4)
                if tail:
                    renorm(pv)
                if front:
                    q_low(nx)
                if front:
                    maxima(nx, 0)
                    maxima(nx, 1)
                if pre:
                    pre_stats(b.after(2))
                w_low(b, 5)
                if tail and b.layer == 1:
                    h2_low(pv)
                if pre and b.layer == 0:
                    mask_flags(b.after(2))
                if front:
                    maxima(nx, 2)
                    maxima(nx, 3)
                w_low(b, 6)
                if tail:
                    if b.layer == 0:
                        route(pv)
                    else:
                        finish(pv)
                if front:
                    maxima(nx, 4)
                    maxima(nx, 5)
                if pre:
                    pre_norm(b.after(2))
                if front:
                    maxima(nx, 6)
                w_low(b, 7)
                if front:
                    maxima(nx, 7)
                normalise(b)
                if ld and b.layer == 1:
                    combine(b.after(3))
                if tail and b.layer == 0:
                    place(pv)
                if pre:
                    if b.layer == 0:
                        mask_rows(b.after(2))
                    v_out(b.after(2))
                if b.layer == 0 and isinstance(b.i, int) and b.i >= 13:
                    part = b.i - 13
                    dve.wait_ge(s.first_high, part + 1)
                    dve.scalar_tensor_tensor(we[:, 0, part, 1], wes[:, 0], SCALE, we[:, 0, part, 0],
                                             ALU.mult, ALU.subtract).then_inc(s.expert_weights, 1)

            dve.wait_ge(s.consts_in, 16)
            dve.tensor_copy(identb[:], ident)
            dve.tensor_copy(utb[:], cst[:, C_UT:C_UT + P])
            dve.tensor_copy(oneb[:], cst[:, C_ONE:C_ONE + P])
            dve.tensor_copy(carry[:], cst[:, C_BASE:C_BASE + E])
            dve.tensor_copy(mhead[:], cst[0:MK, C_MH:C_END].rearrange(
                "p (h k) -> p h k", h=H)).then_inc(s.consts_in, 1)
            dve.wait_ge(s.act_setup, 1)
            dve.tensor_scalar(tgs[:], tg[:], INV, None, ALU.mult)
            for k, g in ((0, 0), (1, 1), (2, 3)):
                dve.tensor_scalar(bias[:, k], bias[:, k], tg[:, g:g + 1], None,
                                  ALU.mult).then_inc(s.dve_setup, 1)
            def weights_rest(k, count):
                dve.wait_ge(s.act_setup, count)
                dve.scalar_tensor_tensor(wat[:, k, 1].rearrange("p c n -> p (c n)"), wst[:, k], SCALE,
                                         wat[:, k, 0].rearrange("p c n -> p (c n)"),
                                         ALU.mult, ALU.subtract).then_inc(s.dve_setup, 1)

            for k in range(NW // 2):
                weights_rest(k, k + 2)
            dve.wait_ge(s.act_setup, NW // 2 + 2)
            dve.tensor_tensor(ctxs[:, 1], ctx32, ctxs[:, 0], ALU.subtract).then_inc(s.dve_setup, 1)
            dve.wait_ge(s.act_setup, NW // 2 + 3)
            dve.scalar_tensor_tensor(bqz[0:1, 1], bqrow[0:1, :], SCALE, bqz[0:1, 0],
                                     ALU.mult, ALU.subtract).then_inc(s.dve_setup, 1)
            dve.wait_ge(s.pool_setup, 8)
            pre_stats(at(0, 0))
            mask_flags(at(0, 0))
            pre_norm(at(0, 0), True)
            mask_rows(at(0, 0), True)
            front_low(at(0, 0))
            pre_stats(at(0, 1))
            v_out(at(0, 0))
            v_low(at(0, 0))
            q_low(at(0, 0))
            v_out(at(0, 1))
            for g in range(GP):
                maxima(at(0, 0), g)
            mask_flags(at(0, 1))
            pre_norm(at(0, 1))
            mask_rows(at(0, 1))
            for k in range(NW // 2, NW):
                weights_rest(k, k + 4)
            steps(dve, 0, step)
            a_low(at(0, 15))
            residual(at(0, 15))
            renorm(at(0, 15))
            route(at(0, 15))
            place(at(0, 15))

            ch = Chain(dve, s.count_step, 19, 0)
            ch.link(dve.tensor_tensor(ntf[:], carry[:], cst[:, C_BASE:C_BASE + E], ALU.subtract))
            ch.link(dve.tensor_scalar(nti[:], ntf[:], float(S - 1), None, ALU.add))
            ch.link(dve.tensor_scalar(nti2[:], nti[:], 8, None, ALU.logical_shift_right))
            ch.link(dve.tensor_scalar(ntf[:], nti2[:], 1.0, None, ALU.max))
            ch.link(dve.memset(tsf[:], 0.0))
            ch.link(dve.memset(eqf[:, 0, 0:E], 1.0))
            ch.link(dve.tensor_tensor_scan(tsf[:, 1:E + 1], eqf[:, 0, 0:E], ntf[:], 0.0,
                                           ALU.mult, ALU.add))
            ch.link(dve.tensor_copy(tbl[0:1, 0:E + 1], tsf[0:1]))
            dve.tensor_copy(tbl[0:1, E + 1:2 * E + 1], carry[0:1, :]).then_inc(s.tiles_counted, 1)
            ch.link(dve.tensor_scalar(shift[:], ntf[:], float(S), -float(CAP), ALU.mult, ALU.add))
            ch.link(dve.tensor_copy(slotx[:], slots[:].rearrange("p b k -> p (b k)")))
            n = NB * QT * 2
            past = h[:].rearrange("p t n -> p (t n)")[:, 0:n * (E - 1)].rearrange("p (n e) -> p n e", n=n)
            ch.link(dve.tensor_tensor(past, slotx[:].unsqueeze(2).to_broadcast([P, n, E - 1]),
                                      cst[:, C_BASE + 1:C_BASE + E].unsqueeze(1).to_broadcast([P, n, E - 1]),
                                      ALU.is_ge))
            ch.link(dve.tensor_tensor(past, past, shift[:, 0:E - 1].unsqueeze(1).to_broadcast([P, n, E - 1]),
                                      ALU.mult))
            ch.link(dve.tensor_reduce(slott[:], past, AX, ALU.add))
            ch.link(dve.tensor_tensor(slotz[:], slotx[:], slott[:], ALU.add))
            ch.link(dve.tensor_copy(slots[:].rearrange("p b k -> p (b k)"), slotz[:]))
            ch.link(dve.memset(wone[:], 0.0))
            dve.tensor_copy(wone[:, 0, 0:1], gap[:, 0, 0:1]).then_inc(s.gap_exponential, 1)
            dve.wait_ge(s.gap_exponential, 2)
            ch.link(dve.tensor_scalar(wone[:], wexp[:], 1.0, None, ALU.add))
            ch.link(dve.reciprocal(wone[:], wone[:]))
            ch.link(dve.tensor_scalar(wtok[:, :, :, 0], wone[:], tg[:, 2:3], None, ALU.mult))
            dve.tensor_tensor(wtok[:, :, :, 1], wtok[:, :, :, 0], wexp[:],
                              ALU.mult).then_inc(s.token_weights, 1)

            dve.wait_ge(s.fourier_read, 3)
            dve.scalar_tensor_tensor(mf[:, 1], b_f[2][:].rearrange("p (c n) -> p c n", c=KC), SCALE / D,
                                     mf[:, 0], ALU.mult, ALU.subtract).then_inc(s.dve_setup, 1)

            dve.memset(ge[:, 0, 0:1], 0.0).then_inc(s.product, FC)
            dve.memset(a32[:, 0, 0:1], 0.0).then_inc(s.down, FC)
            dve.memset(xs[:, 0, 0:1], 0.0).then_inc(s.tile_turned, 1)
            dve.memset(ysb[:, 0, 0:1], 0.0).then_inc(s.expert_rows_stored, 16)
            dve.memset(xT[:, 0, 0, 0:1], 0.0).then_inc(s.expert_rows, 2)
            dve.memset(act16[:, 0, 0, 0:1], 0.0).then_inc(s.credits_given, 1)

            def x_low(g):
                dve.wait_ge(s.tile_high, g + 1)
                dve.tensor_tensor(xT[:, 1], b_t[:].rearrange("p (c n) -> p c n", c=KC), xT[:, 0],
                                  ALU.subtract).then_inc(s.tile_low, 1)

            dve.wait_ge(s.tiles_counted, 1)
            x_low(0)
            with dve.Fori(0, E) as e:
                t0 = dve.value_load(tbl[0:1, bass.ds(e, 1)], min_val=0, max_val=TILES)
                t1 = dve.value_load(tbl[0:1, bass.ds(e + 1, 1)], min_val=1, max_val=TILES)
                with dve.Fori(t0, t1) as g:
                    for fc in range(FC):
                        dve.wait_ge(s.gelu, g * FC + (fc + 1))
                        dve.scalar_tensor_tensor(a32[:, fc % 2], bank[1 + fc % 3][:, S:2 * S], INV,
                                                 ge[:, fc % 2], ALU.mult, ALU.mult).then_inc(s.product, 1)
                        dve.wait_ge(s.product, g * FC + (fc + 9))
                        dve.wait_ge(s.down, g * FC + (fc + 5))
                        dve.tensor_copy(act16[:, fc % 4, 0], a32[:, fc % 2]).then_inc(s.activation, 1)
                        dve.wait_ge(s.activation, g * (2 * FC) + (2 * fc + 1))
                        dve.tensor_tensor(act16[:, fc % 4, 1], a32[:, fc % 2], act16[:, fc % 4, 0],
                                          ALU.subtract).then_inc(s.activation, 1)
                    x_low(g + 1)

            for i in range(3):
                recall(at(1, i))
                if i == 0:
                    dve.wait_ge(s.token_weights, 1)
                if i == 1:
                    combine(at(1, 0))
                    pre_stats(at(1, 0))
                    mask_flags(at(1, 0))
                    mask_rows(at(1, 0))
                    dve.tensor_copy(nfb[:], nf[:]).then_inc(s.unmasked_ready, 1)
                    pre_norm(at(1, 0))
            front_low(at(1, 0))
            v_out(at(1, 0))
            v_low(at(1, 0))
            q_low(at(1, 0))
            v_out(at(1, 1))
            combine(at(1, 1))
            pre_stats(at(1, 1))
            for g in range(GP):
                maxima(at(1, 0), g)
            pre_norm(at(1, 1))
            combine(at(1, 2))
            steps(dve, 1, step)
            a_low(at(1, 15))
            residual(at(1, 15))
            renorm(at(1, 15))
            h2_low(at(1, 15))
            finish(at(1, 15))

        @block.tensor
        def _(pe):
            def turn(dst, src):
                for c in range(KC):
                    for t in range(QT):
                        last = pe.transpose(dst[:, c * S + t * P:c * S + (t + 1) * P],
                                            src[:, t, c * P:(c + 1) * P], ident)
                return last

            def t_h(b):
                pe.wait_ge(s.normed, b.n + 1)
                turn(b_t, h).then_inc(s.normed_turned, 1)

            def t_h2(b):
                pe.wait_ge(s.normed_after, b.n + 1)
                turn(b_t, h2[:, b.par]).then_inc(s.normed_after_turned, 1)

            def proj_q(b):
                pe.wait_ge(s.normed_low, b.n + 1)
                for m in range(KC):
                    n = 0
                    total = 6 + (2 if b.layer else 0)
                    if b.layer:
                        for k in range(2):
                            pe.matmul(b_proj[:, m * S:(m + 1) * S], bqz[:, k, m * P:(m + 1) * P], nfT[:],
                                      start=n == 0, stop=False)
                            n += 1
                    for c in range(KC):
                        for i, j in PASSES:
                            n += 1
                            last = pe.matmul(b_proj[:, m * S:(m + 1) * S],
                                             wat[:, 4 * b.layer, i, c, m * P:(m + 1) * P], hT[:, j, c],
                                             start=n == 1, stop=n == total)
                last.then_inc(s.queries, 1)

            def proj_kv(b):
                for m in range(KC):
                    for n, (c, i, j) in enumerate([(c, i, j) for c in range(KC) for i, j in PASSES]):
                        pe.matmul(b_small[:, m * S2:(m + 1) * S2],
                                  wat[:, 4 * b.layer + 1, i, c, m * P:(m + 1) * P],
                                  ctxs[:, j, c, bass.ds(b.i * S2, S2)], start=n == 0, stop=n == 5)
                for n, (c, i, j) in enumerate([(c, i, j) for c in range(KC) for i, j in PASSES]):
                    last = pe.matmul(b_small[0:S2, 160:416], ctxs[:, i, c, bass.ds(b.i * S2, S2)],
                                     wat[:, 4 * b.layer + 2, j, c], start=n == 0, stop=n == 5)
                last.then_inc(s.keys_values, 1)

            def top_scores(b, g):
                t, q = g // 4, g % 4
                dst = a_place(g)
                if g == 0:
                    pe.wait_ge(s.queries_high, b.n + 1)
                    pe.wait_ge(s.keys_diagonal, 2 * b.n + 1)
                    if not (isinstance(b.n, int) and b.n < 1):
                        pe.wait_ge(s.mask_ready, b.n)
                elif g == 1:
                    pe.wait_ge(s.values_out, b.n + (2 if isinstance(b.i, int) and b.i == 0 else 1))
                else:
                    pe.wait_ge(s.maxima, b.n * GP + (g - 1))
                pe.matmul(dst, qT[:, b.par, 0, q // 2, t * P:(t + 1) * P],
                          kbd[:, b.par, 0, q // 2, 4 * (q % 2):4 * (q % 2) + 4], start=True, stop=False)
                pe.matmul(dst, identb[:], bm[:, t, 0:S2].unsqueeze(1).to_broadcast([P, 4, S2]),
                          start=False, stop=True).then_inc(s.top_scores, 1)

            def t_mask(b):
                pe.wait_ge(s.maxima, GP * (b.n + 1))
                for t in range(QT):
                    last = pe.transpose(b_top[0:MK, 384 + 64 * t:384 + 64 * (t + 1)].bitcast(BF16),
                                        bm[:, t], identb[:])
                last.then_inc(s.mask_turned, 1)

            def scores(b, g):
                if g == 0:
                    pe.wait_ge(s.mask_ready, b.n + 1)
                    pe.wait_ge(s.queries_low, b.n + 1)
                    pe.wait_ge(s.keys_diagonal, 2 * b.n + 2)
                if g >= 2:
                    pe.wait_ge(s.weights, b.n * GP + (g - 1))
                for j in range(2):
                    head = 2 * g + j
                    c, hh = head // HC, head % HC
                    dst = b_s[g % 2][0:S2, j * S:(j + 1) * S]
                    for n, (ki, qi) in enumerate(PASSES):
                        pe.matmul(dst, kbd[:, b.par, ki, c, hh], qT[:, b.par, qi, c],
                                  start=n == 0, stop=False)
                    last = pe.matmul(dst, mhead[:, head], mrhs[:], start=False, stop=True)
                last.then_inc(s.scores, 1)

            def values(b, g):
                if g == 0:
                    pe.wait_ge(s.values_low, b.n + 1)
                    if not (isinstance(b.n, int) and b.n < 1):
                        pe.wait_ge(s.attended, b.n)
                pe.wait_ge(*low_done(b, g))
                for j in range(2):
                    head = 2 * g + j
                    for t in range(QT):
                        for n, (vi, pi) in enumerate(PASSES):
                            last = pe.matmul(b_pv[t][:, head * (DH + 1):(head + 1) * (DH + 1)],
                                             pr[0:S2, g % 4, pi, j * S + t * P:j * S + (t + 1) * P],
                                             vaug[0:S2, b.par, vi, head], start=n == 0, stop=n == 2)
                last.then_inc(s.weighted_values, 1)

            def t_att(b):
                pe.wait_ge(s.attended, b.n + 1)
                turn(b_t, att).then_inc(s.attended_turned, 1)

            def token_major(lhs, weight, done):
                for t in range(QT):
                    for n, (c, i, j) in enumerate([(c, i, j) for c in range(KC) for i, j in PASSES]):
                        last = pe.matmul(b_proj[:, t * D:(t + 1) * D], lhs[:, i, c, t * P:(t + 1) * P],
                                         weight[:, j, c], start=n == 0, stop=n == 5)
                last.then_inc(done, 1)

            def proj_o(b):
                pe.wait_ge(s.attended_low, b.n + 1)
                token_major(aT, wat[:, 4 * b.layer + 3], s.attention_out)

            def logits(b):
                for t in range(QT):
                    for c in range(KC):
                        last = pe.matmul(b_proj[:, t * E:(t + 1) * E], h2T[:, c, t * P:(t + 1) * P],
                                         wg[:, c], start=c == 0, stop=c == KC - 1)
                last.then_inc(s.logits, 1)

            def prefix(b):
                pe.wait_ge(s.picked, b.i + 1)
                pe.matmul(b_proj[:, 16:24], utb[:], pick[:, 0], start=True, stop=True)
                pe.matmul(b_proj[:, 24:32], utb[:], pick[:, 1], start=True, stop=False)
                pe.matmul(b_proj[:, 24:32], oneb[:], pick[:, 0], start=False, stop=True)
                pe.matmul(b_proj[:, 32:40], oneb[:], pick[:, 0], start=True, stop=False)
                pe.matmul(b_proj[:, 32:40], oneb[:], pick[:, 1], start=False, stop=True).then_inc(s.prefix, 1)

            def step(b, front, tail, pre, ld):
                nx, pv = b.after(1), b.after(-1)
                scores(b, 0)
                if tail:
                    t_att(pv)
                scores(b, 1)
                scores(b, 2)
                values(b, 0)
                if front:
                    if tail:
                        pe.wait_ge(s.attended_low, pv.n + 1)
                    t_h(nx)
                scores(b, 3)
                if tail:
                    if not (isinstance(pv.i, int) and pv.i < 1):
                        pe.wait_ge(s.final_rows if b.layer else s.placed, pv.i)
                    proj_o(pv)
                values(b, 1)
                scores(b, 4)
                values(b, 2)
                if front:
                    if tail:
                        pe.wait_ge(s.row_update, pv.n + 1)
                    proj_q(nx)
                scores(b, 5)
                values(b, 3)
                if front:
                    top_scores(nx, 0)
                    top_scores(nx, 1)
                if tail:
                    if front:
                        pe.wait_ge(s.normed_low, nx.n + 1)
                    t_h2(pv)
                scores(b, 6)
                if front:
                    top_scores(nx, 2)
                    top_scores(nx, 3)
                values(b, 4)
                if tail:
                    pe.wait_ge(s.normed_after_high, pv.n + 1)
                    if front:
                        pe.wait_ge(s.queries_low, nx.n + 1)
                    if b.layer == 0:
                        logits(pv)
                    else:
                        pe.wait_ge(s.normed_after_low, pv.i + 1)
                        token_major(h2s, mf, s.fourier_out)
                if front:
                    top_scores(nx, 4)
                    top_scores(nx, 5)
                scores(b, 7)
                values(b, 5)
                if front:
                    top_scores(nx, 6)
                values(b, 6)
                if front:
                    top_scores(nx, 7)
                values(b, 7)
                if tail and b.layer == 0:
                    prefix(pv)
                if front:
                    t_mask(nx)
                if pre:
                    pe.wait_ge(s.maxima, GP * (nx.n + 1))
                    proj_kv(b.after(2))

            pe.wait_ge(s.consts_in, 17)
            pe.wait_ge(s.dve_setup, 3 + NW // 2 + 2)
            b0 = at(0, 0)
            t_h(b0)
            proj_kv(b0)
            proj_q(b0)
            pe.wait_ge(s.values_out, 1)
            proj_kv(at(0, 1))
            for g in range(GP):
                top_scores(b0, g)
            t_mask(b0)
            steps(pe, 0, step)
            last0 = at(0, 15)
            t_att(last0)
            pe.wait_ge(s.placed, NB - 1)
            proj_o(last0)
            t_h2(last0)
            pe.wait_ge(s.normed_after_high, NB)
            logits(last0)
            prefix(last0)

            pe.wait_ge(s.fourier_in, 16 * 5)
            for k, terms in enumerate((((0, 0), (1, 1)), ((1, 0), (0, 2)))):
                for m in range(KC):
                    for n, (c, w, f) in enumerate([(c, w, f) for c in range(KC) for w, f in terms]):
                        last = pe.matmul(b_f[k][:, m * D:(m + 1) * D], wf[:, w, c, m * P:(m + 1) * P],
                                         dft[:, f, c], start=n == 0, stop=n == 3)
                last.then_inc(s.fourier_product, 1)
            pe.wait_ge(s.fourier_read, 2)
            for m in range(KC):
                for n, (c, w) in enumerate([(c, w) for c in range(KC) for w in range(2)]):
                    last = pe.matmul(b_f[2][:, m * D:(m + 1) * D], afT[:, w, c, m * P:(m + 1) * P],
                                     dft[:, (0, 2)[w], c], start=n == 0, stop=n == 3)
            last.then_inc(s.fourier_product, 1)

            pe.wait_ge(s.tiles_counted, 1)
            pe.wait_ge(s.credits_given, 1)

            def t_x(g):
                pe.wait_ge(s.tile_in, g * 16 + 16)
                turn(b_t, xs).then_inc(s.tile_turned, 1)

            gate_up = we

            def up(par, g, fc):
                pe.wait_ge(s.product, g * FC + ((fc + 6) if fc >= 3 else (7, 8, 6)[fc]))
                for half in range(2):
                    col = half * F + fc * P
                    high = [(c, i, 0) for c in range(KC) for i in range(2)]
                    for n, (c, i, j) in enumerate(high + [(c, 0, 1) for c in range(KC)]):
                        if fc == 0 and half == 0 and n == len(high):
                            pe.wait_ge(s.tile_low, g + 1)
                        last = pe.matmul(bank[1 + fc % 3][:, half * S:(half + 1) * S],
                                         gate_up[:, par, c, i, col:col + P], xT[:, j, c],
                                         start=n == 0, stop=n == 5)
                last.then_inc(s.gate_up, 1)

            def down(par, g, fc):
                if fc == 0:
                    pe.wait_ge(s.expert_rows, g * 2 + 2)
                for n, (i, j) in enumerate(PASSES):
                    if n != 1:
                        pe.wait_ge(s.activation, g * (2 * FC) + (2 * fc + 1 + i))
                    for t in range(QT):
                        last = pe.matmul(bank[4 + t][:, 0:D], act16[:, fc % 4, i, t * P:(t + 1) * P],
                                         we[:, par, 2, j, fc * D:(fc + 1) * D],
                                         start=fc == 0 and n == 0, stop=fc == FC - 1 and n == 2)
                last.then_inc(s.down, 1)

            t_x(0)
            with pe.Fori(0, E // 2) as pair:
                for par in range(2):
                    e = pair * 2 + par
                    t0 = pe.value_load(tbl[0:1, bass.ds(e, 1)], min_val=0, max_val=TILES)
                    t1 = pe.value_load(tbl[0:1, bass.ds(e + 1, 1)], min_val=1, max_val=TILES)
                    with pe.Fori(t0, t1) as g:
                        pe.wait_ge(s.expert_weights, e * 3 + 3)
                        pe.wait_ge(s.tile_high, g + 1)
                        up(par, g, 0)
                        up(par, g, 1)
                        for fc in range(2, FC):
                            up(par, g, fc)
                            if fc == 2:
                                t_x(g + 1)
                            down(par, g, fc - 2)
                        down(par, g, FC - 2)
                        down(par, g, FC - 1)

            b1 = at(1, 0)
            proj_kv(b1)
            t_h(b1)
            pe.wait_ge(s.unmasked_ready, 1)
            for t in range(QT):
                last = pe.transpose(b_top[0:1, 384 + 64 * t:384 + 64 * (t + 1)].bitcast(BF16),
                                    nfb[:, t:t + 1], identb[:])
            last.then_inc(s.unmasked_turned, 1)
            pe.wait_ge(s.unmasked_ready, 2)
            proj_q(b1)
            pe.wait_ge(s.values_out, NB + 1)
            proj_kv(at(1, 1))
            for g in range(GP):
                top_scores(b1, g)
            t_mask(b1)
            steps(pe, 1, step)
            last1 = at(1, 15)
            t_att(last1)
            pe.wait_ge(s.final_rows, NB - 1)
            proj_o(last1)
            t_h2(last1)
            pe.wait_ge(s.normed_after_low, NB)
            token_major(h2s, mf, s.fourier_out)


def tables():
    c = np.zeros((P, C_END), np.float32)
    r = np.arange(P)
    c[:, C_ID:C_ID + P] = np.eye(P)
    c[:, C_UT:C_UT + P] = r[:, None] < r[None, :]
    c[:, C_ONE:C_ONE + P] = 1.0
    c[:, C_SEL:C_SEL + HC] = r[:, None] // DH == np.arange(HC)[None, :]
    c[:, C_IOTA:C_IOTA + E] = np.arange(E)
    c[:, C_BASE:C_BASE + E] = np.arange(E) * CAP
    m = np.zeros((P, H, S2), np.float32)
    for k in range(S2):
        m[k, :, k] = 1.0
    for head in range(H):
        m[MROW + head, head, :] = -1.0
    c[:, C_MH:C_END] = m.reshape(P, -1)
    angle = 2.0 * np.pi * (np.outer(np.arange(D), np.arange(D)) % D) / D
    return c, np.cos(angle).astype(np.float32), np.sin(angle).astype(np.float32)


def kernel(**inputs):
    import concourse.bacc as bacc
    from concourse.bass_utils import run_bass_kernel_spmd as run

    arr = {k: np.asarray(v) for k, v in inputs.items()}
    consts, dcos, dsin = tables()
    laid = {
        "x": arr["x"], "mask0": arr["mask_Bx1xSxS2_if1"], "mask1": arr["mask_1x1xSxS2_ik0"],
        "consts": consts, "dcos": dcos, "dsin": dsin, "dnsin": tables()[2] * np.float32(-1),
        "ctxT": arr["ctx_1024"].transpose(2, 0, 1).reshape(D, NB * S2),
        "w0": arr["L0_xattn_Wq"].T, "w1": arr["L0_xattn_Wk"].T,
        "w2": arr["L0_xattn_Wv"].T, "w3": arr["L0_xattn_Wo"].T,
        "w4": arr["L1_xattn_wq_w"].T, "w5": arr["L1_xattn_wk_w"].T,
        "w6": arr["L1_xattn_wv_w"].T, "w7": arr["L1_xattn_wo_w"].T,
        "gates": np.concatenate([arr["g_xattn"], arr["g_ffn"]]),
        "bo0": arr["L0_xattn_bo"], "bo1": arr["L1_xattn_wo_b"], "fb": arr["L1_ffn_bias"],
        "bv": arr["L1_xattn_wv_b"], "bk": arr["L1_xattn_wk_b"].reshape(KC, P).T, "bq": arr["L1_xattn_wq_b"],
        "gwT": arr["L0_ffn_gate_w"].T,
        "guT": arr["L0_ffn_gate_up_w"].transpose(0, 2, 1).reshape(E * D, 2 * F),
        "dnT": arr["L0_ffn_down_w"].transpose(0, 2, 1).reshape(E * F, D),
        "wfr": arr["L1_ffn_w_freq_real"], "wfi": arr["L1_ffn_w_freq_imag"],
    }
    nc = bacc.Bacc("TRN2", target_bir_lowering=False, num_devices=1)
    arrays, args = {}, {}
    for name, value in laid.items():
        value = np.ascontiguousarray(value)
        arrays[f"in_{name}"] = value
        args[name] = nc.dram_tensor(f"in_{name}", value.shape, mybir.dt.from_np(value.dtype),
                                    kind="ExternalInput").ap()
    out = nc.dram_tensor("out_0", (NB, S, D), F32, kind="ExternalOutput").ap()
    build(nc, args, out)
    r = run(nc, [arrays], core_ids=[0])
    return r.results[0]["out_0"]
```
